# Optimizing a Trainium2 kernel written in Bass

```python
import numpy as np
import jax
import jax.numpy as jnp

def _softmax(x, axis=-1):
    return jax.nn.softmax(x, axis=axis)

def _gelu(x):
    return jax.nn.gelu(x, approximate=True)

def _silu(x):
    return jax.nn.silu(x)

def _sigmoid(x):
    return jax.nn.sigmoid(x)

def _layernorm(x, axis=-1, eps=1e-05):
    m = jnp.mean(x, axis=axis, keepdims=True)
    v = jnp.var(x, axis=axis, keepdims=True)
    return (x - m) / jnp.sqrt(v + eps)

def _scatter_add(tgt, idx, src, axis=0):
    return tgt.at[idx].add(src)

def _segment_sum(src, seg, n):
    return jax.ops.segment_sum(src, seg, n)
kernel_name = 'mk_decoder_preln_d1_seqx_r4_1d04b8'

def setup_inputs(seed: int=0):
    np.random.seed(seed)
    _w = jnp.asarray

    def _rec_inputs():
        import jax
        import jax.numpy as jnp
        _rk = jax.random.key(seed)
        x = -0.0002928 + 1 * jax.random.normal(jax.random.fold_in(_rk, 1), (4, 512, 256), jnp.float32)
        _lenS = 512 - jax.random.randint(jax.random.fold_in(_rk, 7), (4,), 0, max(1, 512 // 4) + 1, jnp.int32)
        _lenS2 = 1024 - jax.random.randint(jax.random.fold_in(_rk, 8), (4,), 0, max(1, 1024 // 4) + 1, jnp.int32)
        _ctx_512P = jax.random.normal(jax.random.fold_in(_rk, 11), (4, 16, 128), jnp.float32)
        _ctx_512c = jax.random.dirichlet(jax.random.fold_in(_rk, 511), 0.3 * jnp.ones((16,), jnp.float32), (4, 1024))
        _ctx_512t = jnp.einsum('bsk,bkd->bsd', _ctx_512c, _ctx_512P)
        _ctx_512t = _ctx_512t * jax.lax.rsqrt(jnp.mean(jnp.square(_ctx_512t)) + 1e-12) * 0.953939
        ctx_512 = 0.00222621 + 0.99962 * (_ctx_512t + 0.3 * jax.random.normal(jax.random.fold_in(_rk, 611), (4, 1024, 128), jnp.float32))
        return (x, ctx_512)
    x, ctx_512 = _rec_inputs()

    def _L0_attn_setup():
        import jax, jax.numpy as jnp
        import numpy as np
        B_, L_, D_MODEL = (2, 512, 256)
        D_INNER, D_STATE, D_CONV, DT_RANK = (512, 16, 4, 64)

        def _mamba(hidden_states, in_proj_w, conv_w, conv_b, x_proj_w, dt_proj_w, dt_proj_b, A_log, D, out_proj_w):
            B, L, _ = hidden_states.shape
            xz = jnp.einsum('bld,ed->bel', hidden_states, in_proj_w)
            x, z = jnp.split(xz, 2, axis=1)
            xp = jnp.pad(x, ((0, 0), (0, 0), (D_CONV - 1, 0)))
            xc = jax.lax.conv_general_dilated(xp, conv_w, (1,), 'VALID', dimension_numbers=('NCH', 'OIH', 'NCH'), feature_group_count=D_INNER)
            x = jax.nn.silu(xc + conv_b[None, :, None])
            x_dbl = jnp.einsum('bdl,kd->bkl', x, x_proj_w)
            dt_in = x_dbl[:, :DT_RANK]
            Bm = x_dbl[:, DT_RANK:DT_RANK + D_STATE]
            Cm = x_dbl[:, DT_RANK + D_STATE:]
            delta = jnp.einsum('brl,dr->bdl', dt_in, dt_proj_w)
            delta = jax.nn.softplus(delta + dt_proj_b[None, :, None])
            A = -jnp.exp(A_log)
            dA = jnp.exp(jnp.einsum('bdl,dn->lbdn', delta, A))
            dBu = jnp.einsum('bdl,bnl,bdl->lbdn', delta, Bm, x)
            C_t = jnp.transpose(Cm, (2, 0, 1))

            def step(h, inp):
                dA_t, dBu_t, c_t = inp
                h = dA_t * h + dBu_t
                y = jnp.einsum('bdn,bn->bd', h, c_t)
                return (h, y)
            h0 = jnp.zeros((B, D_INNER, D_STATE), delta.dtype)
            _, ys = jax.lax.scan(step, h0, (dA, dBu, C_t))
            y = jnp.transpose(ys, (1, 2, 0))
            y = y + x * D[None, :, None]
            y = y * jax.nn.silu(z)
            return jnp.einsum('bdl,od->blo', y, out_proj_w)
        key = jax.random.key(seed)
        ks = jax.random.split(key, 8)
        hidden_states = jax.random.normal(ks[0], (B_, L_, D_MODEL), jnp.float32)
        in_proj_w = jax.random.normal(ks[1], (2 * D_INNER, D_MODEL), jnp.float32) * D_MODEL ** (-0.5)
        conv_w = jax.random.normal(ks[2], (D_INNER, 1, D_CONV), jnp.float32) * D_CONV ** (-0.5)
        conv_b = jnp.zeros((D_INNER,), jnp.float32)
        x_proj_w = jax.random.normal(ks[3], (DT_RANK + 2 * D_STATE, D_INNER), jnp.float32) * D_INNER ** (-0.5)
        dt_std = DT_RANK ** (-0.5)
        dt_proj_w = jax.random.uniform(ks[4], (D_INNER, DT_RANK), jnp.float32, -dt_std, dt_std)
        dt = jnp.exp(jax.random.uniform(ks[5], (D_INNER,), jnp.float32) * (np.log(0.1) - np.log(0.001)) + np.log(0.001))
        dt_proj_b = dt + jnp.log(-jnp.expm1(-dt))
        A_log = jnp.log(jnp.broadcast_to(jnp.arange(1, D_STATE + 1, dtype=jnp.float32), (D_INNER, D_STATE)))
        D = jnp.ones((D_INNER,), jnp.float32)
        out_proj_w = jax.random.normal(ks[6], (D_MODEL, D_INNER), jnp.float32) * D_INNER ** (-0.5)
        return dict(hidden_states=hidden_states, in_proj_w=in_proj_w, conv_w=conv_w, conv_b=conv_b, x_proj_w=x_proj_w, dt_proj_w=dt_proj_w, dt_proj_b=dt_proj_b, A_log=A_log, D=D, out_proj_w=out_proj_w)
    _L0_attn_all = _L0_attn_setup()
    _L0_attn_in = {k: v for k, v in _L0_attn_all.items() if k in ('in_proj_w', 'conv_w', 'conv_b', 'x_proj_w', 'dt_proj_w', 'dt_proj_b', 'A_log', 'D', 'out_proj_w')}
    del _L0_attn_all

    def _L0_xattn_setup():
        import jax, jax.numpy as jnp
        import numpy as np
        B, T, TC, C, CC, H = (2, 512, 128, 256, 128, 16)
        D = C // H

        def _heads(t):
            b, l, _ = t.shape
            return t.reshape(b, l, H, D).transpose(0, 2, 1, 3)
        key = jax.random.key(seed)
        ks = jax.random.split(key, 18)
        w = lambda k, i, o: jax.random.normal(k, (i, o), jnp.float32) / np.sqrt(i).astype(np.float32)
        return {'x': jax.random.normal(ks[0], (B, T, C), jnp.float32), 'cross_input': jax.random.normal(ks[1], (B, TC, CC), jnp.float32), 'Wk': w(ks[2], C, C), 'bk': jnp.zeros((C,), jnp.float32), 'Wq': w(ks[3], C, C), 'bq': jnp.zeros((C,), jnp.float32), 'Wv': w(ks[4], C, C), 'bv': jnp.zeros((C,), jnp.float32), 'Wck': w(ks[5], CC, C), 'bck': jnp.zeros((C,), jnp.float32), 'Wcq': w(ks[6], C, C), 'bcq': jnp.zeros((C,), jnp.float32), 'Wcv': w(ks[7], CC, C), 'bcv': jnp.zeros((C,), jnp.float32), 'Wp': w(ks[8], C, C), 'bp': jnp.zeros((C,), jnp.float32)}
    _L0_xattn_all = _L0_xattn_setup()
    _L0_xattn_in = {k: v for k, v in _L0_xattn_all.items() if k in ('Wk', 'bk', 'Wq', 'bq', 'Wv', 'bv', 'Wck', 'bck', 'Wcq', 'bcq', 'Wcv', 'bcv', 'Wp', 'bp')}
    del _L0_xattn_all

    def _L0_ffn_setup():
        import jax, jax.numpy as jnp
        import numpy as np
        from jax.scipy.linalg import expm
        B, S, D, E, K, NROT = (2, 512, 256, 8, 2, 3)
        EPS = 1e-05

        def _gelu(x):
            return jax.nn.gelu(x, approximate=False)

        def _forward(x, ln_gamma, ln_beta, abel_w, abel_b, moe_gate_w, moe_gate_b, ew1, eb1, ew2, eb2, gens, gc_w, gc_b):
            residual = x
            mu = jnp.mean(x, axis=-1, keepdims=True)
            var = jnp.mean((x - mu) ** 2, axis=-1, keepdims=True)
            xn = (x - mu) * jax.lax.rsqrt(var + EPS) * ln_gamma + ln_beta
            abel_out = _gelu(xn @ abel_w + abel_b)
            logits = xn @ moe_gate_w + moe_gate_b
            topw, topi = jax.lax.top_k(logits, K)
            topw = jax.nn.softmax(topw, axis=-1)
            w_dense = jnp.sum(jax.nn.one_hot(topi, E, dtype=xn.dtype) * topw[..., None], axis=-2)
            h = _gelu(jnp.einsum('bsd,edh->ebsh', xn, ew1) + eb1[:, None, None, :])
            eo = jnp.einsum('ebsh,ehd->ebsd', h, ew2) + eb2[:, None, None, :]
            moe_out = jnp.einsum('ebsd,bse->bsd', eo, w_dense)
            for i in range(NROT):
                moe_out = moe_out @ expm(gens[i])
            combined = jnp.concatenate([abel_out, moe_out], axis=-1)
            gate = jax.nn.sigmoid(combined @ gc_w + gc_b)
            mixed = abel_out * (1.0 - gate) + moe_out * gate
            return residual + mixed
        key = jax.random.key(seed)
        ks = jax.random.split(key, 16)
        sc = 0.02
        x = jax.random.normal(ks[0], (B, S, D), jnp.float32)
        ln_gamma = 1.0 + sc * jax.random.normal(ks[1], (D,), jnp.float32)
        ln_beta = sc * jax.random.normal(ks[2], (D,), jnp.float32)
        abel_w = sc * jax.random.normal(ks[3], (D, D), jnp.float32)
        abel_b = sc * jax.random.normal(ks[4], (D,), jnp.float32)
        moe_gate_w = sc * jax.random.normal(ks[5], (D, E), jnp.float32)
        moe_gate_b = sc * jax.random.normal(ks[6], (E,), jnp.float32)
        ew1 = sc * jax.random.normal(ks[7], (E, D, 2 * D), jnp.float32)
        eb1 = sc * jax.random.normal(ks[8], (E, 2 * D), jnp.float32)
        ew2 = sc * jax.random.normal(ks[9], (E, 2 * D, D), jnp.float32)
        eb2 = sc * jax.random.normal(ks[10], (E, D), jnp.float32)
        g = sc * jax.random.normal(ks[11], (NROT, D, D), jnp.float32)
        gens = 0.5 * (g - jnp.swapaxes(g, -1, -2))
        gc_w = sc * jax.random.normal(ks[12], (2 * D, 1), jnp.float32)
        gc_b = sc * jax.random.normal(ks[13], (1,), jnp.float32)
        return dict(x=x, ln_gamma=ln_gamma, ln_beta=ln_beta, abel_w=abel_w, abel_b=abel_b, moe_gate_w=moe_gate_w, moe_gate_b=moe_gate_b, ew1=ew1, eb1=eb1, ew2=ew2, eb2=eb2, gens=gens, gc_w=gc_w, gc_b=gc_b)
    _L0_ffn_all = _L0_ffn_setup()
    _L0_ffn_in = {k: v for k, v in _L0_ffn_all.items() if k in ('ln_gamma', 'ln_beta', 'abel_w', 'abel_b', 'moe_gate_w', 'moe_gate_b', 'ew1', 'eb1', 'ew2', 'eb2', 'gens', 'gc_w', 'gc_b')}
    del _L0_ffn_all
    return {'x': x, 'ctx_512': ctx_512, 'L0_attn_in_proj_w': _L0_attn_in['in_proj_w'], 'L0_attn_conv_w': _L0_attn_in['conv_w'], 'L0_attn_conv_b': _L0_attn_in['conv_b'], 'L0_attn_x_proj_w': _L0_attn_in['x_proj_w'], 'L0_attn_dt_proj_w': _L0_attn_in['dt_proj_w'], 'L0_attn_dt_proj_b': _L0_attn_in['dt_proj_b'], 'L0_attn_A_log': _L0_attn_in['A_log'], 'L0_attn_D': _L0_attn_in['D'], 'L0_attn_out_proj_w': _L0_attn_in['out_proj_w'], 'L0_xattn_Wk': _L0_xattn_in['Wk'], 'L0_xattn_bk': _L0_xattn_in['bk'], 'L0_xattn_Wq': _L0_xattn_in['Wq'], 'L0_xattn_bq': _L0_xattn_in['bq'], 'L0_xattn_Wv': _L0_xattn_in['Wv'], 'L0_xattn_bv': _L0_xattn_in['bv'], 'L0_xattn_Wck': _L0_xattn_in['Wck'], 'L0_xattn_bck': _L0_xattn_in['bck'], 'L0_xattn_Wcq': _L0_xattn_in['Wcq'], 'L0_xattn_bcq': _L0_xattn_in['bcq'], 'L0_xattn_Wcv': _L0_xattn_in['Wcv'], 'L0_xattn_bcv': _L0_xattn_in['bcv'], 'L0_xattn_Wp': _L0_xattn_in['Wp'], 'L0_xattn_bp': _L0_xattn_in['bp'], 'L0_ffn_ln_gamma': _L0_ffn_in['ln_gamma'], 'L0_ffn_ln_beta': _L0_ffn_in['ln_beta'], 'L0_ffn_abel_w': _L0_ffn_in['abel_w'], 'L0_ffn_abel_b': _L0_ffn_in['abel_b'], 'L0_ffn_moe_gate_w': _L0_ffn_in['moe_gate_w'], 'L0_ffn_moe_gate_b': _L0_ffn_in['moe_gate_b'], 'L0_ffn_ew1': _L0_ffn_in['ew1'], 'L0_ffn_eb1': _L0_ffn_in['eb1'], 'L0_ffn_ew2': _L0_ffn_in['ew2'], 'L0_ffn_eb2': _L0_ffn_in['eb2'], 'L0_ffn_gens': _L0_ffn_in['gens'], 'L0_ffn_gc_w': _L0_ffn_in['gc_w'], 'L0_ffn_gc_b': _L0_ffn_in['gc_b']}

def reference(x, ctx_512, L0_attn_in_proj_w, L0_attn_conv_w, L0_attn_conv_b, L0_attn_x_proj_w, L0_attn_dt_proj_w, L0_attn_dt_proj_b, L0_attn_A_log, L0_attn_D, L0_attn_out_proj_w, L0_xattn_Wk, L0_xattn_bk, L0_xattn_Wq, L0_xattn_bq, L0_xattn_Wv, L0_xattn_bv, L0_xattn_Wck, L0_xattn_bck, L0_xattn_Wcq, L0_xattn_bcq, L0_xattn_Wcv, L0_xattn_bcv, L0_xattn_Wp, L0_xattn_bp, L0_ffn_ln_gamma, L0_ffn_ln_beta, L0_ffn_abel_w, L0_ffn_abel_b, L0_ffn_moe_gate_w, L0_ffn_moe_gate_b, L0_ffn_ew1, L0_ffn_eb1, L0_ffn_ew2, L0_ffn_eb2, L0_ffn_gens, L0_ffn_gc_w, L0_ffn_gc_b):
    import jax
    import jax.numpy as jnp

    def _L0_attn_ref(hidden_states, in_proj_w, conv_w, conv_b, x_proj_w, dt_proj_w, dt_proj_b, A_log, D, out_proj_w):
        import jax, jax.numpy as jnp
        import numpy as np
        B_, L_, D_MODEL = (2, 512, 256)
        D_INNER, D_STATE, D_CONV, DT_RANK = (512, 16, 4, 64)

        def _mamba(hidden_states, in_proj_w, conv_w, conv_b, x_proj_w, dt_proj_w, dt_proj_b, A_log, D, out_proj_w):
            B, L, _ = hidden_states.shape
            xz = jnp.einsum('bld,ed->bel', hidden_states, in_proj_w)
            x, z = jnp.split(xz, 2, axis=1)
            xp = jnp.pad(x, ((0, 0), (0, 0), (D_CONV - 1, 0)))
            xc = jax.lax.conv_general_dilated(xp, conv_w, (1,), 'VALID', dimension_numbers=('NCH', 'OIH', 'NCH'), feature_group_count=D_INNER)
            x = jax.nn.silu(xc + conv_b[None, :, None])
            x_dbl = jnp.einsum('bdl,kd->bkl', x, x_proj_w)
            dt_in = x_dbl[:, :DT_RANK]
            Bm = x_dbl[:, DT_RANK:DT_RANK + D_STATE]
            Cm = x_dbl[:, DT_RANK + D_STATE:]
            delta = jnp.einsum('brl,dr->bdl', dt_in, dt_proj_w)
            delta = jax.nn.softplus(delta + dt_proj_b[None, :, None])
            A = -jnp.exp(A_log)
            dA = jnp.exp(jnp.einsum('bdl,dn->lbdn', delta, A))
            dBu = jnp.einsum('bdl,bnl,bdl->lbdn', delta, Bm, x)
            C_t = jnp.transpose(Cm, (2, 0, 1))

            def step(h, inp):
                dA_t, dBu_t, c_t = inp
                h = dA_t * h + dBu_t
                y = jnp.einsum('bdn,bn->bd', h, c_t)
                return (h, y)
            h0 = jnp.zeros((B, D_INNER, D_STATE), delta.dtype)
            _, ys = jax.lax.scan(step, h0, (dA, dBu, C_t))
            y = jnp.transpose(ys, (1, 2, 0))
            y = y + x * D[None, :, None]
            y = y * jax.nn.silu(z)
            return jnp.einsum('bdl,od->blo', y, out_proj_w)
        return _mamba(hidden_states, in_proj_w, conv_w, conv_b, x_proj_w, dt_proj_w, dt_proj_b, A_log, D, out_proj_w)

    def _L0_xattn_ref(x, cross_input, Wk, bk, Wq, bq, Wv, bv, Wck, bck, Wcq, bcq, Wcv, bcv, Wp, bp):
        import jax, jax.numpy as jnp
        import numpy as np
        B, T, TC, C, CC, H = (2, 512, 128, 256, 128, 16)
        D = C // H

        def _heads(t):
            b, l, _ = t.shape
            return t.reshape(b, l, H, D).transpose(0, 2, 1, 3)
        scale = np.float32(1.0 / np.sqrt(D))
        q = _heads(x @ Wq + bq)
        k = _heads(x @ Wk + bk)
        v = _heads(x @ Wv + bv)
        att = jnp.einsum('bhqd,bhkd->bhqk', q, k) * scale
        causal = jnp.tril(jnp.ones((T, T), bool))
        att = jnp.where(causal[None, None], att, -jnp.inf)
        y = jnp.einsum('bhqk,bhkd->bhqd', jax.nn.softmax(att, axis=-1), v)
        qc = _heads(x @ Wcq + bcq)
        kc = _heads(cross_input @ Wck + bck)
        vc = _heads(cross_input @ Wcv + bcv)
        attc = jnp.einsum('bhqd,bhkd->bhqk', qc, kc) * scale
        y = y + jnp.einsum('bhqk,bhkd->bhqd', jax.nn.softmax(attc, axis=-1), vc)
        y = y.transpose(0, 2, 1, 3).reshape(x.shape[0], T, C)
        return y @ Wp + bp

    def _L0_ffn_ref(x, ln_gamma, ln_beta, abel_w, abel_b, moe_gate_w, moe_gate_b, ew1, eb1, ew2, eb2, gens, gc_w, gc_b):
        import jax, jax.numpy as jnp
        import numpy as np
        from jax.scipy.linalg import expm
        B, S, D, E, K, NROT = (2, 512, 256, 8, 2, 3)
        EPS = 1e-05

        def _gelu(x):
            return jax.nn.gelu(x, approximate=False)

        def _forward(x, ln_gamma, ln_beta, abel_w, abel_b, moe_gate_w, moe_gate_b, ew1, eb1, ew2, eb2, gens, gc_w, gc_b):
            residual = x
            mu = jnp.mean(x, axis=-1, keepdims=True)
            var = jnp.mean((x - mu) ** 2, axis=-1, keepdims=True)
            xn = (x - mu) * jax.lax.rsqrt(var + EPS) * ln_gamma + ln_beta
            abel_out = _gelu(xn @ abel_w + abel_b)
            logits = xn @ moe_gate_w + moe_gate_b
            topw, topi = jax.lax.top_k(logits, K)
            topw = jax.nn.softmax(topw, axis=-1)
            w_dense = jnp.sum(jax.nn.one_hot(topi, E, dtype=xn.dtype) * topw[..., None], axis=-2)
            h = _gelu(jnp.einsum('bsd,edh->ebsh', xn, ew1) + eb1[:, None, None, :])
            eo = jnp.einsum('ebsh,ehd->ebsd', h, ew2) + eb2[:, None, None, :]
            moe_out = jnp.einsum('ebsd,bse->bsd', eo, w_dense)
            for i in range(NROT):
                moe_out = moe_out @ expm(gens[i])
            combined = jnp.concatenate([abel_out, moe_out], axis=-1)
            gate = jax.nn.sigmoid(combined @ gc_w + gc_b)
            mixed = abel_out * (1.0 - gate) + moe_out * gate
            return residual + mixed
        return _forward(x, ln_gamma, ln_beta, abel_w, abel_b, moe_gate_w, moe_gate_b, ew1, eb1, ew2, eb2, gens, gc_w, gc_b)
    x = x + _L0_attn_ref(_layernorm(x, axis=-1), L0_attn_in_proj_w, L0_attn_conv_w, L0_attn_conv_b, L0_attn_x_proj_w, L0_attn_dt_proj_w, L0_attn_dt_proj_b, L0_attn_A_log, L0_attn_D, L0_attn_out_proj_w)
    x = x + _L0_xattn_ref(_layernorm(x, axis=-1), ctx_512, L0_xattn_Wk, L0_xattn_bk, L0_xattn_Wq, L0_xattn_bq, L0_xattn_Wv, L0_xattn_bv, L0_xattn_Wck, L0_xattn_bck, L0_xattn_Wcq, L0_xattn_bcq, L0_xattn_Wcv, L0_xattn_bcv, L0_xattn_Wp, L0_xattn_bp)
    x = x + _L0_ffn_ref(_layernorm(x, axis=-1), L0_ffn_ln_gamma, L0_ffn_ln_beta, L0_ffn_abel_w, L0_ffn_abel_b, L0_ffn_moe_gate_w, L0_ffn_moe_gate_b, L0_ffn_ew1, L0_ffn_eb1, L0_ffn_ew2, L0_ffn_eb2, L0_ffn_gens, L0_ffn_gc_w, L0_ffn_gc_b)
    return x

_drawn_inputs = setup_inputs


def setup_inputs(seed=0):
    import zlib

    import numpy as np

    out = dict(_drawn_inputs(seed))
    spreads = {'L0_attn_conv_b': (0.0, 0.1),
     'L0_attn_D': (1.0, 0.2),
     'L0_xattn_bk': (0.0, 2.0),
     'L0_xattn_bq': (0.0, 0.668),
     'L0_xattn_bv': (0.0, 0.1),
     'L0_xattn_bck': (0.0, 2.0),
     'L0_xattn_bcq': (0.0, 0.456),
     'L0_xattn_bcv': (0.0, 0.1),
     'L0_xattn_bp': (0.0, 0.1)}
    factors = {'L0_ffn_ln_gamma': 8.0,
     'L0_ffn_ln_beta': 8.0,
     'L0_ffn_abel_b': 28.685,
     'L0_ffn_moe_gate_w': 4.825,
     'L0_ffn_moe_gate_b': 8.0,
     'L0_ffn_ew1': 4.594,
     'L0_ffn_eb1': 8.0,
     'L0_ffn_ew2': 4.476,
     'L0_ffn_eb2': 29.657,
     'L0_ffn_gens': 8.0,
     'L0_ffn_gc_w': 8.0}
    for name, (base, spread) in spreads.items():
        noise = np.random.default_rng([zlib.crc32(name.encode()), seed]).standard_normal(out[name].shape)
        drawn = base * np.exp(spread * noise) if base else spread * noise
        out[name] = jnp.asarray(drawn.astype(out[name].dtype))
    for name, factor in factors.items():
        out[name] = (out[name] * factor).astype(out[name].dtype)
    return out
```

```python
import concourse.bass as bass
from concourse import mybir
from contextlib import ExitStack
from math import factorial

F32 = mybir.dt.float32
BF16 = mybir.dt.bfloat16
ALU = mybir.AluOpType
ACT = mybir.ActivationFunctionType
AXX = mybir.AxisListType.X

P = 128
NB, T, DM = 4, 512, 256
TC, CC = 1024, 128
TT = T // P
KM = DM // P
DI, NS, DCONV, RK = 512, 16, 4, 64
DT = DI // P
H, HD = 16, 16
HG = 4
NG = H // HG
VW = 32
SK = 6 * HD
SR = SK + 3
NPAR = 3
NE, HID = 8, 512
HT = HID // P
NGEN, SQUARINGS = 3, 6
EPS = 1e-5
MASKED = -1e30
Q_PART = [0, 0, 0, 1, 1, 2]
K_RUNS = [(0, 3), (3, 2), (5, 1)]


def decoder(nc, w, x_in, ctx_t, out):
    qkv_dram = nc.dram_tensor("stack_parts", (4, 3, H, HD, TC), BF16).ap()
    with ExitStack() as ctx:
        sems = []

        def sb(name, shape, dt=F32):
            return ctx.enter_context(nc.sbuf_tensor(name, shape, dt))

        def sem(name):
            s = ctx.enter_context(nc.semaphore(name))
            sems.append(s)
            return s

        PS = ctx.enter_context(nc.psum_tensor("PS", [P, 8, 512], F32))

        def bank(i):
            return PS[:, i, :]

        in_w = sb("in_w", [P, KM, 2 * DI])
        conv_w = sb("conv_w", [P, DT, DCONV])
        conv_b = sb("conv_b", [P, DT])
        xproj_w = sb("xproj_w", [P, DT, RK + 2 * NS])
        dt_w = sb("dt_w", [RK, DI])
        dt_b = sb("dt_b", [P, DT])
        A_neg = sb("A_neg", [P, DT, NS])
        D_skip = sb("D_skip", [P, DT])
        out_w = sb("out_w", [P, DT, DM])
        wq = sb("wq", [P, KM, DM])
        wk = sb("wk", [P, KM, DM])
        wv = sb("wv", [P, KM, DM])
        wcq = sb("wcq", [P, KM, DM])
        wck = sb("wck", [P, DM])
        wcv = sb("wcv", [P, DM])
        bqk = sb("bqk", [P, 4, KM])
        bv = sb("bv", [P, DM])
        bcv = sb("bcv", [P, DM])
        wp = sb("wp", [P, NG, DM])
        bp = sb("bp", [P, DM])
        gam = sb("gam", [P, KM])
        bet = sb("bet", [P, KM])
        abw = sb("abw", [P, KM, DM + NE])
        abb = sb("abb", [P, DM + NE])
        eb1 = sb("eb1", [P, NE, HT])
        eb2 = sb("eb2", [NE, DM])
        gcw = sb("gcw", [P, 2 * DM])
        gcb = sb("gcb", [P, 1])
        Wrot = sb("Wrot", [P, KM, DM])
        ident = sb("ident", [P, P])
        identb = sb("identb", [P, P], BF16)
        mask_qk = sb("mask_qk", [P, P], BF16)
        mask_kq = sb("mask_kq", [P, P], BF16)
        den_sel = sb("den_sel", [P, P])
        bc_sel = sb("bc_sel", [6 * NS, 2 * NS, P], BF16)
        eps_t = sb("eps_t", [P, 1])
        x_sb = sb("x_sb", [P, TT, DM])
        x1 = sb("x1", [P, TT, DM])
        xn = sb("xn", [P, TT, DM])
        xT = sb("xT", [P, KM, T])
        ctxT = sb("ctxT", [P, TC])
        stats = sb("stats", [P, TT, 6])
        mv = sb("mv", [P, TT, 2])
        rs = sb("rs", [P, 4, TT])
        dtin = sb("dtin", [RK, T])
        bc3 = sb("bc3", [6 * NS, T], BF16)
        bcr = sb("bcr", [2 * NS, 2, T])
        maxs = sb("maxs", [P, 2, TT, 2 * HG])
        mparts = sb("mparts", [2 * HG, 2, 3, T], BF16)
        mrest = sb("mrest", [2 * HG, T])
        m8 = sb("m8", [P, TT, 8])
        sel = sb("sel", [P, TT, NE])
        sel_ex = sb("sel_ex", [P, TT, NE])
        sel_e2 = sb("sel_e2", [P, TT, 1])
        s_gt = sb("s_gt", [P, TT, NE])
        s_eq = sb("s_eq", [P, TT, NE])
        s_one = sb("s_one", [P, TT, 1])
        s_zero = sb("s_zero", [P, NE])
        s_den = sb("s_den", [P, TT, 1])
        selT = sb("selT", [NE, T])
        gate = sb("gate", [P, 3, TT])
        NAR = 29696
        arena = sb("arena", [P, NAR])
        used = [0]

        def ar(n, dt=F32):
            words = n if dt == F32 else n // 2
            v = arena[:, used[0]:used[0] + words]
            used[0] += words
            assert used[0] <= NAR, used[0]
            return v if dt == F32 else v.bitcast(dt)

        def ar_start(at=0):
            used[0] = at

        def mm(o, l, r, start, stop):
            return nc.tensor.matmul(o, l, r, start=start, stop=stop)

        def reset():
            engines = (nc.gpsimd, nc.scalar, nc.sync, nc.vector)
            for i, s in enumerate(sems):
                engines[i % 4].sem_clear(s)
            nc.all_engine_barrier()

        load_w = sem("load_w")
        load_a = sem("load_a")
        load_gen = sem("load_gen")
        const_ready = sem("const_ready")
        id_ready = sem("id_ready")
        exp_mm = sem("exp_mm")
        exp_ev = sem("exp_ev")
        a_ready = sem("a_ready")
        pool_chain = sem("pool_chain")
        dve_chain = sem("dve_chain")
        act_chain = sem("act_chain")

        def chain(eng, s):
            count = [0]

            def link(ins):
                count[0] += 1
                ins.then_inc(s, 1)
                eng.wait_ge(s, count[0])
            link.sem, link.count = s, count
            return link

        ar_start()
        G = [{n: ar(KM * DM).rearrange("p (k n) -> p k n", k=KM)
              for n in ("A", "T", "A2", "A3", "X")} for _ in range(NGEN)]
        Iw = ar(KM * DM).rearrange("p (k n) -> p k n", k=KM)
        A_raw = ar(DT * NS).rearrange("p (k n) -> p k n", k=DT)
        coef = [1.0 / factorial(i) for i in range(13)]
        N_STEPS = 4 + 1 + 3 + 2 * SQUARINGS
        with nc.Block() as block:
            @block.sync
            def _(sp):
                for g in range(NGEN):
                    sp.dma_start(G[g]["A"], w["gens"][g].rearrange("(k p) n -> p k n", p=P)).then_inc(load_gen, 16)
                sp.dma_start(A_raw, w["A_log"].rearrange("(k p) n -> p k n", p=P)).then_inc(load_a, 16)
                n = 0
                loads = [
                    (in_w[:], w["in_proj_wT"].rearrange("(k p) n -> p k n", p=P)),
                    (conv_w[:], w["conv_w"].rearrange("(k p) n -> p k n", p=P)),
                    (conv_b[:], w["conv_b"]),
                    (xproj_w[:], w["x_proj_wT"].rearrange("(k p) n -> p k n", p=P)),
                    (dt_w[:], w["dt_proj_wT"]),
                    (dt_b[:], w["dt_proj_b"]),
                    (D_skip[:], w["D"]),
                    (out_w[:], w["out_proj_wT"].rearrange("(k p) n -> p k n", p=P)),
                    (wq[:], w["Wq"].rearrange("(k p) n -> p k n", p=P)),
                    (wk[:], w["Wk"].rearrange("(k p) n -> p k n", p=P)),
                    (wv[:], w["Wv"].rearrange("(k p) n -> p k n", p=P)),
                    (wcq[:], w["Wcq"].rearrange("(k p) n -> p k n", p=P)),
                    (wck[:], w["Wck"]),
                    (wcv[:], w["Wcv"]),
                    (bqk[:, 0, :], w["bq"]),
                    (bqk[:, 1, :], w["bk"]),
                    (bqk[:, 2, :], w["bcq"]),
                    (bqk[:, 3, :], w["bck"]),
                    (bv[:], w["bv"].partition_broadcast(P)),
                    (bcv[:], w["bcv"].partition_broadcast(P)),
                    (bp[:], w["bp"].partition_broadcast(P)),
                    (gam[:], w["ln_gamma"]),
                    (bet[:], w["ln_beta"]),
                    (abw[:, :, 0:DM], w["abel_w"].rearrange("(k p) n -> p k n", p=P)),
                    (abw[:, :, DM:DM + NE], w["moe_gate_w"].rearrange("(k p) n -> p k n", p=P)),
                    (abb[:, 0:DM], w["abel_b"].partition_broadcast(P)),
                    (abb[:, DM:DM + NE], w["moe_gate_b"].partition_broadcast(P)),
                    (eb1[:], w["eb1"]),
                    (eb2[:], w["eb2"]),
                    (gcw[:], w["gc_w"].rearrange("n o -> (n o)").partition_broadcast(P)),
                    (gcb[:], w["gc_b"].partition_broadcast(P)),
                ]
                for o, i in loads:
                    sp.dma_start(o, i).then_inc(load_w, 16)
                    n += 16
                sp.wait_ge(const_ready, 1)
                for g in range(NG):
                    for j in range(HG):
                        r = (g * HG + j) * HD
                        sp.dma_start(wp[32 * j:32 * j + HD, g, :], w["Wp"][r:r + HD, :]).then_inc(load_w, 16)
                        n += 16
                sp.wait_ge(load_w, n)

            @block.gpsimd
            def _(pool):
                link = chain(pool, pool_chain)
                nc.gpsimd.memset(ident[:], 0.0).then_inc(id_ready, 1)
                pool.wait_ge(id_ready, 1)
                nc.gpsimd.affine_select(out=ident[:], in_=ident[:], compare_op=ALU.not_equal, fill=1.0, base=0,
                                        pattern=[[-1, P]], channel_multiplier=1).then_inc(id_ready, 1)
                nc.gpsimd.memset(wp[:], 0.0).then_inc(const_ready, 1)
                link(nc.gpsimd.memset(Iw, 0.0))
                for k in range(KM):
                    link(nc.gpsimd.affine_select(out=Iw[:, k, :], in_=Iw[:, k, :], compare_op=ALU.not_equal, fill=1.0,
                                                 base=k * P, pattern=[[-1, DM]], channel_multiplier=1))
                pool.wait_ge(id_ready, 2)
                link(nc.gpsimd.tensor_copy(identb[:], ident[:]))
                link(nc.gpsimd.memset(mask_qk[:], 0.0))
                link(nc.gpsimd.memset(mask_kq[:], 0.0))
                link(nc.gpsimd.affine_select(out=mask_qk[:], in_=mask_qk[:], compare_op=ALU.is_ge, fill=MASKED, base=0,
                                             pattern=[[-1, P]], channel_multiplier=1))
                link(nc.gpsimd.affine_select(out=mask_kq[:], in_=mask_kq[:], compare_op=ALU.is_ge, fill=MASKED, base=0,
                                             pattern=[[1, P]], channel_multiplier=-1))
                link(nc.gpsimd.memset(den_sel[:], 0.0))
                v = den_sel[:].rearrange("p (a c) -> p a c", c=32)
                link(nc.gpsimd.affine_select(out=v, in_=v, compare_op=ALU.not_equal, fill=1.0, base=-HD,
                                             pattern=[[-32, 4], [0, 32]], channel_multiplier=1))
                link(nc.gpsimd.memset(bc_sel[:], 0.0))
                for part in range(3):
                    link(nc.gpsimd.affine_select(out=bc_sel[:], in_=bc_sel[:], compare_op=ALU.not_equal, fill=1.0,
                                                 base=-32 * part, pattern=[[-1, 2 * NS], [0, P]], channel_multiplier=1))
                nc.gpsimd.memset(eps_t[:], EPS).then_inc(const_ready, 1)

            @block.scalar
            def _(act):
                act.wait_ge(load_a, 16)
                nc.scalar.activation(A_neg[:], A_raw, ACT.Exp).then_inc(a_ready, 1)

            @block.tensor
            def _(pe):
                step = [0]

                def ready(g):
                    pe.wait_ge(exp_ev, NGEN * step[0] + g + 1)

                def o3(g):
                    return bank(g).rearrange("p (k n) -> p k n", k=KM)

                def product(lT, r):
                    for g in range(NGEN):
                        ready(g)
                        for m in range(KM):
                            for k in range(KM):
                                last = mm(o3(g)[:, m, :], G[g][lT][:, k, m * P:(m + 1) * P], G[g][r][:, k, :],
                                          k == 0, k == KM - 1)
                        last.then_inc(exp_mm, 1)
                    step[0] += 1

                def transposed(s):
                    for g in range(NGEN):
                        ready(g)
                        for m in range(KM):
                            for k in range(KM):
                                last = nc.tensor.transpose(o3(g)[:, m, k * P:(k + 1) * P],
                                                           G[g][s][:, k, m * P:(m + 1) * P], ident[:])
                        last.then_inc(exp_mm, 1)
                    step[0] += 1

                pe.wait_ge(id_ready, 2)
                transposed("A")
                product("T", "A")
                product("T", "A2")
                transposed("A3")
                for _ in range(3):
                    product("T", "X")
                for s in range(SQUARINGS):
                    transposed("X")
                    if s < SQUARINGS - 1:
                        product("T", "X")
                for g in range(NGEN):
                    ready(g)
                    lT, r = ("T", "X") if g == NGEN - 1 else ("X", "T")
                    for m in range(KM):
                        for k in range(KM):
                            last = mm(o3(g)[:, m, :], G[g][lT][:, k, m * P:(m + 1) * P], G[g][r][:, k, :],
                                      k == 0, k == KM - 1)
                    last.then_inc(exp_mm, 1)
                step[0] += 1
                for i, (g, r) in enumerate(((1, G[2]["X"]), (0, G[2]["T"]))):
                    pe.wait_ge(exp_ev, NGEN * (step[0] + 1) + i)
                    for m in range(KM):
                        for k in range(KM):
                            last = mm(o3(i)[:, m, :], G[g]["X"][:, k, m * P:(m + 1) * P], r[:, k, :],
                                      k == 0, k == KM - 1)
                    last.then_inc(exp_mm, 1)

            @block.vector
            def _(dve):
                link = chain(dve, dve_chain)
                done = [0]

                def o3(g):
                    return bank(g).rearrange("p (k n) -> p k n", k=KM)

                def product_ready():
                    done[0] += 1
                    dve.wait_ge(exp_mm, done[0])

                def evac(dst):
                    for g in range(NGEN):
                        product_ready()
                        nc.vector.tensor_copy(G[g][dst], o3(g)).then_inc(exp_ev, 1)

                for g in range(NGEN):
                    dve.wait_ge(load_gen, 16 * (g + 1))
                dve.wait_ge(a_ready, 1)
                link(nc.vector.tensor_scalar(A_neg[:], A_neg[:], -1.0, None, ALU.mult))
                for g in range(NGEN):
                    nc.vector.tensor_scalar(G[g]["A"], G[g]["A"], 2.0 ** -SQUARINGS, None,
                                            ALU.mult).then_inc(exp_ev, 1)
                evac("T")
                evac("A2")
                dve.wait_ge(pool_chain, 3)
                for g in range(NGEN):
                    product_ready()
                    nc.vector.tensor_copy(G[g]["A3"], o3(g)).then_inc(exp_ev, 1)
                for g in range(NGEN):
                    X, A, A2, A3 = (G[g][n] for n in ("X", "A", "A2", "A3"))
                    product_ready()
                    link(nc.vector.tensor_copy(G[g]["T"], o3(g)))
                    link(nc.vector.tensor_scalar(X, A3, coef[12], None, ALU.mult))
                    link(nc.vector.scalar_tensor_tensor(X, A2, coef[11], X, ALU.mult, ALU.add))
                    link(nc.vector.scalar_tensor_tensor(X, A, coef[10], X, ALU.mult, ALU.add))
                    nc.vector.scalar_tensor_tensor(X, Iw, coef[9], X, ALU.mult, ALU.add).then_inc(exp_ev, 1)
                for i in (6, 3, 0):
                    for g in range(NGEN):
                        X, A, A2 = (G[g][n] for n in ("X", "A", "A2"))
                        product_ready()
                        link(nc.vector.scalar_tensor_tensor(X, A2, coef[i + 2], o3(g), ALU.mult, ALU.add))
                        link(nc.vector.scalar_tensor_tensor(X, A, coef[i + 1], X, ALU.mult, ALU.add))
                        nc.vector.scalar_tensor_tensor(X, Iw, coef[i], X, ALU.mult, ALU.add).then_inc(exp_ev, 1)
                for s in range(SQUARINGS):
                    evac("T")
                    evac("X")
                product_ready()
                nc.vector.tensor_copy(G[2]["T"], o3(0)).then_inc(exp_ev, 1)
                product_ready()
                nc.vector.tensor_copy(Wrot[:], o3(1)).then_inc(exp_ev, 1)
        reset()

        names = """load_x load_ctx xn_ready ln_var ln_y0 xT_mm xT_ready inproj_mm xp_ready xc_ready xs_ready z_ready
            xdbl_mm dtin_ready bc_hi bc3_ready dt_mm sp_ready
            bc_mm bn_copied b_ready a_done h_done g_done y_mm
            gated outproj_mm bp_added qkv_mm hi_f_ready mid_ready parts_ready v_mm v_init v_ready
            ones_ready max_mm max_done mt_mm mparts_ready score_mm probs_ready pv_mm pv_copied den_mm norm_ready
            y_ready wp_mm res_added hid_mm hid_ready eo_mm eo_added ab_mm abel_pre abel_ready sel_d sel_e sel_ready
            wT_mm wT_ready eb_mm moe_init moeT_mm moeT_ready rot_mm gate_z gate_e out_ready stored dve_chain1 act_chain1 dve_chain2 dve_chain3 act_chain3
            pool_chain4 dve_chain4 act_chain5 dve_chain5""".split()
        S = {n: sem(n) for n in names}
        parts_stored = [sem(f"parts_stored{i}") for i in range(4)]
        stack_in = [sem(f"stack_in{g}") for g in range(NG)]
        max_rows = [sem(f"max_rows{g}") for g in range(NG)]
        load_e = [sem(f"load_e{e}") for e in range(NE)]

        def four(n=T):
            return ar(DT * n).rearrange("p (k n) -> p k n", k=DT)

        def stack(n):
            return ar(HG * n, BF16).rearrange("p (h n) -> p h n", h=HG)

        ar_start()
        delta, u, xs, zs = four(), four(), four(), four()
        scan_at = used[0]
        xp, xc, tmp = four(T + 4), four(), four()
        ar_start(scan_at)
        a_sb = [four(), four()]
        b_sb = [four(), four()]
        g_sb = [four(), four()]
        h_sb = [four(), four()]
        Bn = [ar(T), ar(T)]
        ar_start(scan_at)
        f_sb = [ar(T), ar(T)]
        r_sb = [ar(T), ar(T)]
        pt = [ar(3 * T, BF16).rearrange("p (k n) -> p k n", k=3) for _ in range(4)]
        pre_at = used[0]
        V = ar(TT * H * VW).rearrange("p (t h d) -> p t h d", t=TT, h=H)
        VC = ar(2 * TT * H * VW).rearrange("p (t h d) -> p t h d", t=2 * TT, h=H)
        KC = [stack(TC) for _ in range(NPAR)]
        NPR = 8
        probs = [ar(T) for _ in range(NPR)]
        ar_start()
        Q = [stack(T) for _ in range(NPAR)]
        K = [stack(T) for _ in range(NPAR)]
        C = [stack(T) for _ in range(NPAR)]
        YT = [ar(T) for _ in range(NG)]
        yt_end = used[0]
        Y1, Y2, R1, R2 = ar(T), ar(T), ar(T), ar(T)
        assert used[0] <= pre_at
        ar_start()
        hid = [four(), four()]
        ab = ar(TT * (DM + NE)).rearrange("p (t n) -> p t n", t=TT)
        acc = ar(TT * DM).rearrange("p (t n) -> p t n", t=TT)
        moeT = ar(KM * T).rearrange("p (k n) -> p k n", k=KM)
        assert used[0] <= NPAR * 3 * HG * T // 2
        ar_start(yt_end)
        xn2 = ar(TT * DM).rearrange("p (t n) -> p t n", t=TT)
        mixed = ar(TT * DM).rearrange("p (t n) -> p t n", t=TT)
        assert used[0] <= pre_at
        ar_start(pre_at)
        ew1 = [ar(KM * HID).rearrange("p (k n) -> p k n", k=KM) for _ in range(NE)]
        ew2 = [ar(HT * DM).rearrange("p (k n) -> p k n", k=HT) for _ in range(NE)]

        def normalise(dve, link, src, dst, i, n):
            for t in range(TT):
                nc.vector.bn_stats(out=stats[:, t, :], in_=src[:, t, :]).then_inc(link.sem, 1)
            link.count[0] += TT
            dve.wait_ge(link.sem, link.count[0])
            for t in range(TT):
                nc.vector.bn_aggr(out=mv[:, t, :], in_=stats[:, t, :]).then_inc(link.sem, 1)
            link.count[0] += TT
            dve.wait_ge(link.sem, link.count[0])
            nc.vector.tensor_scalar(rs[:, 0, :], mv[:, :, 1], EPS, None, ALU.add).then_inc(S["ln_var"], 1)
            dve.wait_ge(S["ln_y0"], n)
            dve.wait_ge(S["ln_var"], n)
            link(nc.vector.tensor_tensor(rs[:, 3, :], rs[:, 2, :], rs[:, 2, :], ALU.mult))
            link(nc.vector.tensor_tensor(rs[:, 3, :], rs[:, 3, :], rs[:, 0, :], ALU.mult))
            link(nc.vector.tensor_scalar(rs[:, 3, :], rs[:, 3, :], -0.5, 1.5, ALU.mult, ALU.add))
            link(nc.vector.tensor_tensor(rs[:, 2, :], rs[:, 2, :], rs[:, 3, :], ALU.mult))
            for t in range(TT):
                nc.vector.tensor_scalar(dst[:, t, :], src[:, t, :], mv[:, t, 0:1], rs[:, 2, t:t + 1],
                                        ALU.subtract, ALU.mult).then_inc(S["xn_ready"], 1)

        def inverse_root(act, link, n):
            act.wait_ge(S["ln_var"], n)
            link(nc.scalar.activation(rs[:, 1, :], rs[:, 0, :], ACT.Ln))
            nc.scalar.activation(rs[:, 2, :], rs[:, 1, :], ACT.Exp, scale=-0.5).then_inc(S["ln_y0"], 1)

        def to_columns(pe, src, n, b0):
            for t in range(TT):
                pe.wait_ge(S["xn_ready"], n + t + 1)
                for k in range(KM):
                    last = nc.tensor.transpose(bank(b0 + k)[:, t * P:(t + 1) * P], src[:, t, k * P:(k + 1) * P],
                                               ident[:])
                    if t == TT - 1:
                        last.then_inc(S["xT_mm"], 1)

        def tok(t):
            return slice(t * P, (t + 1) * P)

        with nc.Fori(0, NB) as b:
            with nc.Block() as block:
                @block.sync
                def _(sp):
                    sp.dma_start(x_sb[:], x_in[bass.ds(b, 1), :, :].rearrange("a (t p) n -> p (a t) n", p=P))\
                        .then_inc(S["load_x"], 16)
                    sp.dma_start(ctxT[:], ctx_t[bass.ds(b, 1), :, :].rearrange("a c n -> (a c) n"))\
                        .then_inc(S["load_ctx"], 16)

                @block.tensor
                def _(pe):
                    to_columns(pe, xn, 0, 0)
                    pe.wait_ge(S["xT_ready"], 2)
                    for m in range(2 * DT):
                        if m == 6:
                            pass
                        for k in range(KM):
                            last = mm(bank((2 + m) % 8), in_w[:, k, m * P:(m + 1) * P], xT[:, k, :], k == 0, k == KM - 1)
                        last.then_inc(S["inproj_mm"], 1)
                    for k in range(DT):
                        pe.wait_ge(S["xs_ready"], k + 1)
                        last = mm(bank(2)[0:RK + 2 * NS], xproj_w[:, k, :], xs[:, k, :], k == 0, k == DT - 1)
                    last.then_inc(S["xdbl_mm"], 1)
                    pe.wait_ge(S["dtin_ready"], 1)
                    for m in range(DT):
                        mm(bank(4 + m), dt_w[:, m * P:(m + 1) * P], dtin[:], True, True).then_inc(S["dt_mm"], 1)

                @block.scalar
                def _(act):
                    link = chain(act, S["act_chain1"])
                    inverse_root(act, link, 1)
                    act.wait_ge(S["xT_mm"], 2)
                    nc.scalar.activation(xT[:, 0, :], bank(0), ACT.Copy).then_inc(S["xT_ready"], 1)
                    for m in range(DT):
                        act.wait_ge(S["inproj_mm"], m + 1)
                        nc.scalar.activation(xp[:, m, 3:3 + T], bank(2 + m), ACT.Copy).then_inc(S["xp_ready"], 1)
                    for m in range(DT):
                        act.wait_ge(S["inproj_mm"], DT + m + 1)
                        nc.scalar.activation(zs[:, m, :], bank((6 + m) % 8), ACT.Silu).then_inc(S["z_ready"], 1)
                    for m in range(DT):
                        act.wait_ge(S["xc_ready"], m + 1)
                        nc.scalar.activation(xs[:, m, :], xc[:, m, :], ACT.Silu).then_inc(S["xs_ready"], 1)
                    act.wait_ge(S["xdbl_mm"], 1)
                    nc.scalar.activation(dtin[:], bank(2)[0:RK], ACT.Copy).then_inc(S["dtin_ready"], 1)
                    nc.scalar.activation(bc3[0:2 * NS], bank(2)[RK:RK + 2 * NS], ACT.Copy).then_inc(S["bc_hi"], 1)
                    for m in range(DT):
                        act.wait_ge(S["dt_mm"], m + 1)
                        nc.scalar.activation(delta[:, m, :], bank(4 + m), ACT.Identity, bias=dt_b[:, m:m + 1])
                        ins = nc.scalar.activation(tmp[:, m, :], bank(4 + m), ACT.Abs, bias=dt_b[:, m:m + 1])
                    link(ins)
                    link(nc.scalar.activation(tmp, tmp, ACT.Exp, scale=-1.0))
                    nc.scalar.activation(tmp, tmp, ACT.Ln, bias=1.0).then_inc(S["sp_ready"], 1)

                @block.vector
                def _(dve):
                    link = chain(dve, S["dve_chain1"])
                    dve.wait_ge(S["load_x"], 16)
                    normalise(dve, link, x_sb, xn, 0, 1)
                    link(nc.vector.memset(xp[:, :, 0:3], 0.0))
                    dve.wait_ge(S["xT_mm"], 2)
                    nc.vector.tensor_copy(xT[:, 1, :], bank(1)).then_inc(S["xT_ready"], 1)
                    for m in range(DT):
                        dve.wait_ge(S["xp_ready"], m + 1)
                        link(nc.vector.tensor_scalar(xc[:, m, :], xp[:, m, 0:T], conv_w[:, m, 0:1], conv_b[:, m:m + 1],
                                                     ALU.mult, ALU.add))
                        for j in range(1, DCONV):
                            ins = nc.vector.scalar_tensor_tensor(xc[:, m, :], xp[:, m, j:j + T], conv_w[:, m, j:j + 1],
                                                                 xc[:, m, :], ALU.mult, ALU.add)
                            if j < DCONV - 1:
                                link(ins)
                        ins.then_inc(S["xc_ready"], 1)
                    dve.wait_ge(S["bc_hi"], 1)
                    link(nc.vector.tensor_tensor(bcr[:, 0, :], bank(2)[RK:RK + 2 * NS], bc3[0:2 * NS], ALU.subtract))
                    nc.vector.tensor_copy(bc3[2 * NS:4 * NS], bcr[:, 0, :]).then_inc(S["bc3_ready"], 1)
                    mid = bcr[:, 1, :].bitcast(BF16)[:, 0:T]
                    link(nc.vector.tensor_copy(mid, bcr[:, 0, :]))
                    nc.vector.tensor_tensor(bc3[4 * NS:6 * NS], bcr[:, 0, :], mid, ALU.subtract)\
                        .then_inc(S["bc3_ready"], 1)
                    dve.wait_ge(S["sp_ready"], 1)
                    link(nc.vector.scalar_tensor_tensor(delta, delta, 0.0, tmp, ALU.max, ALU.add))
                    link(nc.vector.tensor_tensor(u, delta, xs, ALU.mult))

            with nc.Block() as block:
                @block.tensor
                def _(pe):
                    def sum_states(n):
                        pe.wait_ge(S["g_done"], n + 1)
                        for k in range(DT):
                            last = mm(bank(k), ident[:], g_sb[n % 2][:, k, :], n == 0, n == NS - 1)
                        last.then_inc(S["y_mm"], 1)

                    for n in range(NS):
                        if n >= 2:
                            pe.wait_ge(S["bn_copied"], n - 1)
                        mm(bank(4 + n % 2), bc_sel[:, n, :], bc3[:], True, True)
                        if n >= 2:
                            pe.wait_ge(S["g_done"], n - 1)
                        mm(bank(6 + n % 2), bc_sel[:, NS + n, :], bc3[:], True, True).then_inc(S["bc_mm"], 1)
                        if n >= 1:
                            sum_states(n - 1)
                    sum_states(NS - 1)

                @block.scalar
                def _(act):
                    for n in range(NS):
                        act.wait_ge(S["bc_mm"], n + 1)
                        if n >= 2:
                            act.wait_ge(S["b_ready"], n - 1)
                        nc.scalar.activation(Bn[n % 2], bank(4 + n % 2), ACT.Copy).then_inc(S["bn_copied"], 1)
                        if n >= 2:
                            act.wait_ge(S["h_done"], n - 1)
                        for k in range(DT):
                            last = nc.scalar.activation(a_sb[n % 2][:, k, 1:T], delta[:, k, 1:T], ACT.Exp,
                                                        scale=A_neg[:, k, n:n + 1])
                        last.then_inc(S["a_done"], 1)

                @block.gpsimd
                def _(pool):
                    for n in range(NS):
                        pool.wait_ge(S["bn_copied"], n + 1)
                        if n >= 2:
                            pool.wait_ge(S["h_done"], n - 1)
                        nc.gpsimd.tensor_tensor(b_sb[n % 2], u, Bn[n % 2].unsqueeze(1).to_broadcast([P, DT, T]),
                                                ALU.mult).then_inc(S["b_ready"], 1)

                @block.vector
                def _(dve):
                    link = chain(dve, S["dve_chain2"])
                    flat = "p k n -> p (k n)"
                    for i in range(2):
                        link(nc.vector.memset(a_sb[i][:, :, 0:1], 0.0))
                    for n in range(NS):
                        dve.wait_ge(S["a_done"], n + 1)
                        dve.wait_ge(S["b_ready"], n + 1)
                        if n >= 2:
                            dve.wait_ge(S["g_done"], n - 1)
                        nc.vector.tensor_tensor_scan(h_sb[n % 2].rearrange(flat), a_sb[n % 2].rearrange(flat),
                                                     b_sb[n % 2].rearrange(flat), 0.0, ALU.mult, ALU.add)\
                            .then_inc(S["h_done"], 1)
                        dve.wait_ge(S["h_done"], n + 1)
                        if n >= 2:
                            dve.wait_ge(S["y_mm"], n - 1)
                        nc.vector.tensor_tensor(g_sb[n % 2], h_sb[n % 2],
                                                bank(6 + n % 2).unsqueeze(1).to_broadcast([P, DT, T]), ALU.mult)\
                            .then_inc(S["g_done"], 1)

            TILES = [(0, 0, 0), (0, 1, 0), (1, 0, 0), (1, 1, 0), (2, 0, 0), (2, 1, 0),
                     (3, 0, 0), (3, 0, 1), (3, 1, 0), (3, 1, 1)]
            with nc.Block() as block:
                @block.sync
                def _(sp):
                    for i, (x, hh, half) in enumerate(TILES):
                        sp.wait_ge(S["parts_ready"], i + 1)
                        dst = qkv_dram[x, :, 8 * hh:8 * hh + 8, :, half * T:(half + 1) * T]
                        sp.dma_start(dst.rearrange("j h d t -> (h d) j t"), pt[i % 4]).then_inc(parts_stored[i % 4], 16)
                    for i in range(4):
                        sp.wait_ge(parts_stored[i], 16 * len(range(i, len(TILES), 4)))

                @block.tensor
                def _(pe):
                    for t in range(TT):
                        for k in range(DT):
                            pe.wait_ge(S["gated"], k + 1)
                            last = mm(bank(4 + t)[:, 0:DM], u[:, k, tok(t)], out_w[:, k, :], k == 0, k == DT - 1)
                        last.then_inc(S["outproj_mm"], 1)
                    to_columns(pe, xn, TT, 0)
                    pe.wait_ge(S["xT_ready"], 4)
                    pe.wait_ge(S["load_ctx"], 16)
                    ws = [wq, wk, wcq]
                    nv = [0]

                    def value_tile():
                        t = nv[0]
                        if t >= 2:
                            pe.wait_ge(S["v_ready"], t - 1)
                        o = bank(t % 2)[:, 0:DM]
                        if t < TT:
                            for k in range(KM):
                                last = mm(o, xT[:, k, tok(t)], wv[:, k, :], k == 0, k == KM - 1)
                        else:
                            last = mm(o, ctxT[:, tok(t - TT)], wcv[:], True, True)
                        last.then_inc(S["v_mm"], 1)
                        nv[0] += 1

                    for i, (x, hh, half) in enumerate(TILES):
                        if i >= 6:
                            pe.wait_ge(S["hi_f_ready"], i - 5)
                        o = bank(2 + i % 6)
                        cols = slice(hh * P, (hh + 1) * P)
                        if x < 3:
                            for k in range(KM):
                                last = mm(o, ws[x][:, k, cols], xT[:, k, :], k == 0, k == KM - 1)
                        else:
                            last = mm(o, wck[:, cols], ctxT[:, half * T:(half + 1) * T], True, True)
                        last.then_inc(S["qkv_mm"], 1)
                        value_tile()
                    value_tile()
                    value_tile()

                @block.scalar
                def _(act):
                    link = chain(act, S["act_chain3"])
                    inverse_root(act, link, 2)
                    act.wait_ge(S["xT_mm"], 4)
                    nc.scalar.activation(xT[:, 0, :], bank(0), ACT.Copy).then_inc(S["xT_ready"], 1)
                    for i, (x, hh, half) in enumerate(TILES):
                        act.wait_ge(S["qkv_mm"], i + 1)
                        if i >= 4:
                            act.wait_ge(parts_stored[i % 4], 16 * (i // 4))
                        if i >= 2:
                            act.wait_ge(S["mid_ready"], i - 1)
                        bias = bqk[:, x, hh:hh + 1]
                        nc.scalar.activation(pt[i % 4][:, 0, :], bank(2 + i % 6), ACT.Identity, bias=bias)
                        nc.scalar.activation(f_sb[i % 2], bank(2 + i % 6), ACT.Identity, bias=bias)\
                            .then_inc(S["hi_f_ready"], 1)

                @block.gpsimd
                def _(pool):
                    nc.gpsimd.memset(V, 0.0).then_inc(S["v_init"], 1)
                    nc.gpsimd.memset(VC, 0.0).then_inc(S["v_init"], 1)
                    pool.wait_ge(S["v_init"], 2)
                    nc.gpsimd.memset(V[:, :, :, HD:HD + 1], 1.0)
                    nc.gpsimd.memset(VC[:, :, :, HD:HD + 1], 1.0).then_inc(S["v_init"], 1)
                    pool.wait_ge(S["xn_ready"], 2 * TT)
                    nc.gpsimd.tensor_tensor(x1[:], x1[:], bp[:].unsqueeze(1).to_broadcast([P, TT, DM]), ALU.add)\
                        .then_inc(S["bp_added"], 1)
                    for i in range(len(TILES)):
                        pool.wait_ge(S["mid_ready"], i + 1)
                        nc.gpsimd.tensor_tensor(pt[i % 4][:, 2, :], r_sb[i % 2], pt[i % 4][:, 1, :], ALU.subtract)\
                            .then_inc(S["parts_ready"], 1)

                @block.vector
                def _(dve):
                    link = chain(dve, S["dve_chain3"])
                    for k in range(DT):
                        link(nc.vector.scalar_tensor_tensor(delta[:, k, :], xs[:, k, :], D_skip[:, k:k + 1], bank(k),
                                                            ALU.mult, ALU.add))
                        nc.vector.tensor_tensor(u[:, k, :], delta[:, k, :], zs[:, k, :], ALU.mult)\
                            .then_inc(S["gated"], 1)
                    for t in range(TT):
                        dve.wait_ge(S["outproj_mm"], t + 1)
                        link(nc.vector.tensor_tensor(x1[:, t, :], x_sb[:, t, :], bank(4 + t)[:, 0:DM], ALU.add))
                    normalise(dve, link, x1, xn, 1, 2)
                    dve.wait_ge(S["xT_mm"], 4)
                    nc.vector.tensor_copy(xT[:, 1, :], bank(1)).then_inc(S["xT_ready"], 1)
                    dve.wait_ge(S["v_init"], 3)
                    nv = [0]

                    def value_tile():
                        t = nv[0]
                        dve.wait_ge(S["v_mm"], t + 1)
                        dst, bias = (V[:, t, :, 0:HD], bv) if t < TT else (VC[:, t - TT, :, 0:HD], bcv)
                        heads = "p (h d) -> p h d"
                        nc.vector.tensor_tensor(dst, bank(t % 2)[:, 0:DM].rearrange(heads, h=H),
                                                bias[:].rearrange(heads, h=H), ALU.add).then_inc(S["v_ready"], 1)
                        nv[0] += 1

                    for i in range(len(TILES)):
                        dve.wait_ge(S["hi_f_ready"], i + 1)
                        if i >= 2:
                            dve.wait_ge(S["parts_ready"], i - 1)
                        link(nc.vector.tensor_tensor(r_sb[i % 2], f_sb[i % 2], pt[i % 4][:, 0, :], ALU.subtract))
                        nc.vector.tensor_copy(pt[i % 4][:, 1, :], r_sb[i % 2]).then_inc(S["mid_ready"], 1)
                        value_tile()
                    value_tile()
                    value_tile()

            CS = 2 * TT
            STEPS = CS + TT
            JOBS = HG * (TT + 2)
            with nc.Block() as block:
                @block.sync
                def _(sp):
                    k_part = [p for _j, n in K_RUNS for p in range(n)]

                    def load_stacks(g):
                        if g >= NPAR:
                            sp.wait_ge(S["pv_mm"], STEPS * (g - NPAR + 1))
                        heads = slice(g * HG, (g + 1) * HG)
                        for x, dst, parts, n in ((0, Q, Q_PART, T), (1, K, k_part, T), (2, C, Q_PART, T),
                                                 (3, KC, k_part, TC)):
                            for j, part in enumerate(parts):
                                sp.dma_start(dst[g % NPAR][j * HD:(j + 1) * HD],
                                             qkv_dram[x, part, heads, :, 0:n].rearrange("h d t -> d h t"))\
                                    .then_inc(stack_in[g], 16)

                    def load_max_rows(g):
                        sp.wait_ge(S["mparts_ready"], g + 1)
                        for j in range(3):
                            for side, dst in enumerate((Q, C)):
                                sp.dma_start(dst[g % NPAR][SK + j:SK + j + 1],
                                             mparts[side * HG:(side + 1) * HG, g % 2, j, :])\
                                    .then_inc(max_rows[g], 16)

                    for g in range(NPAR):
                        load_stacks(g)
                    load_max_rows(0)
                    load_max_rows(1)
                    load_stacks(3)
                    load_max_rows(2)
                    load_max_rows(3)

                @block.gpsimd
                def _(pool):
                    for i in range(NPAR):
                        nc.gpsimd.memset(K[i][SK:SR], 1.0).then_inc(S["ones_ready"], 1)
                        nc.gpsimd.memset(KC[i][SK:SR], 1.0).then_inc(S["ones_ready"], 1)
                    link = chain(pool, S["pool_chain4"])
                    for g in range(NG):
                        pool.wait_ge(S["norm_ready"], g + 1)
                        link(nc.gpsimd.tensor_tensor(Y1, Y1, R1, ALU.mult))
                        link(nc.gpsimd.tensor_tensor(Y2, Y2, R2, ALU.mult))
                        nc.gpsimd.tensor_tensor(YT[g], Y1, Y2, ALU.add).then_inc(S["y_ready"], 1)

                @block.tensor
                def _(pe):
                    def max_job(g, i):
                        J = JOBS * g + i
                        h, r, s, par = i // (TT + 2), i % (TT + 2), i % 2, g % NPAR
                        if J >= 2:
                            pe.wait_ge(S["max_done"], J - 1)
                        if i < 2 and g >= 1:
                            pe.wait_ge(S["mparts_ready"], g)
                        if r < TT:
                            for c in range(2):
                                last = mm(bank(2 * s + c), C[par][0:SK, h, tok(r)],
                                          KC[par][0:SK, h, c * T:(c + 1) * T], True, True)
                        else:
                            for c, q in enumerate((3, 0) if r == TT else (2, 1)):
                                mm(bank(2 * s + c)[:, 0:(q + 1) * P], Q[par][0:SK, h, tok(q)],
                                   K[par][0:SK, h, 0:(q + 1) * P], True, False)
                                last = mm(bank(2 * s + c)[:, tok(q)], identb[:], mask_qk[:], False, True)
                        last.then_inc(S["max_mm"], 1)

                    def max_rows_out(g):
                        pe.wait_ge(S["max_done"], JOBS * (g + 1))
                        for q in range(TT):
                            last = nc.tensor.transpose(bank(0)[0:2 * HG, tok(q)], maxs[:, g % 2, q, :], ident[:])
                        last.then_inc(S["mt_mm"], 1)

                    def scores(g, k):
                        par = g % NPAR
                        for h in range(HG):
                            n = HG * (STEPS * g + k) + h
                            if n >= 2:
                                pe.wait_ge(S["probs_ready"], n - 1)
                            o = bank(4 + n % 2)
                            if k < CS:
                                last = mm(o, KC[par][0:SR, h, tok(k)], C[par][0:SR, h, :], True, True)
                            else:
                                kt = k - CS
                                mm(o[:, 0:T - kt * P], K[par][0:SR, h, tok(kt)], Q[par][0:SR, h, kt * P:T],
                                   True, False)
                                last = mm(o[:, 0:P], identb[:], mask_kq[:], False, True)
                            last.then_inc(S["score_mm"], 1)

                    def values(g, k):
                        pe.wait_ge(S["probs_ready"], HG * (STEPS * g + k + 1))
                        if k == 0 and g >= 1:
                            pe.wait_ge(S["norm_ready"], g)
                        for h in range(HG):
                            n = HG * (STEPS * g + k) + h
                            rows = slice(32 * h, 32 * h + VW)
                            if k < CS:
                                last = mm(bank(6)[rows], VC[:, k, HG * g + h, :], probs[n % NPR], k == 0, k == CS - 1)
                            else:
                                kt = k - CS
                                last = mm(bank(7)[rows, kt * P:T], V[:, kt, HG * g + h, :],
                                          probs[n % NPR][:, 0:T - kt * P], kt == 0, kt == TT - 1)
                        last.then_inc(S["pv_mm"], 1)

                    n_stack = 16 * 4 * 6
                    pe.wait_ge(stack_in[0], n_stack)
                    for i in range(JOBS):
                        max_job(0, i)
                    max_rows_out(0)
                    pe.wait_ge(S["ones_ready"], 2 * NPAR)
                    for g in range(NG):
                        pe.wait_ge(max_rows[g], 16 * 6)
                        if g + 1 < NG:
                            pe.wait_ge(stack_in[g + 1], n_stack)
                        for k in range(STEPS):
                            scores(g, k)
                            if g + 1 < NG:
                                max_job(g + 1, 2 * k)
                                max_job(g + 1, 2 * k + 1)
                            if k >= 1:
                                values(g, k - 1)
                        values(g, STEPS - 1)
                        if g + 1 < NG:
                            max_rows_out(g + 1)
                        pe.wait_ge(S["pv_copied"], g + 1)
                        mm(bank(6), den_sel[:], Y1, True, True)
                        mm(bank(7), den_sel[:], Y2, True, True).then_inc(S["den_mm"], 1)

                @block.scalar
                def _(act):
                    for s in range(NG * STEPS):
                        k = s % STEPS
                        N = T if k < CS else T - (k - CS) * P
                        if s >= 2:
                            act.wait_ge(S["pv_mm"], s - 1)
                        for h in range(HG):
                            n = HG * s + h
                            act.wait_ge(S["score_mm"], n + 1)
                            nc.scalar.activation(probs[n % NPR][:, 0:N], bank(4 + n % 2)[:, 0:N], ACT.Exp,
                                                 scale=HD ** -0.5).then_inc(S["probs_ready"], 1)

                @block.vector
                def _(dve):
                    link = chain(dve, S["dve_chain4"])

                    def maxima(g):
                        for i in range(JOBS):
                            J = JOBS * g + i
                            h, r, s = i // (TT + 2), i % (TT + 2), i % 2
                            dve.wait_ge(S["max_mm"], J + 1)
                            if r < TT:
                                last = nc.vector.reduce_max(maxs[:, g % 2, r, HG + h:HG + h + 1],
                                                            PS[:, 2 * s:2 * s + 2, :].rearrange("p a n -> p (a n)"), AXX)
                            else:
                                for c_, q in enumerate((3, 0) if r == TT else (2, 1)):
                                    last = nc.vector.reduce_max(maxs[:, g % 2, q, h:h + 1],
                                                                bank(2 * s + c_)[:, 0:(q + 1) * P], AXX)
                            last.then_inc(S["max_done"], 1)

                    def negated_parts(g):
                        dve.wait_ge(S["mt_mm"], g + 1)
                        if g >= 2:
                            dve.wait_ge(max_rows[g - 2], 16 * 6)
                        m = mparts[:, g % 2]
                        src = bank(0)[0:2 * HG]
                        link(nc.vector.tensor_scalar(m[:, 0, :], src, -1.0, None, ALU.mult))
                        link(nc.vector.scalar_tensor_tensor(mrest[:], src, -1.0, m[:, 0, :], ALU.mult, ALU.subtract))
                        link(nc.vector.tensor_copy(m[:, 1, :], mrest[:]))
                        nc.vector.tensor_tensor(m[:, 2, :], mrest[:], m[:, 1, :], ALU.subtract)\
                            .then_inc(S["mparts_ready"], 1)

                    maxima(0)
                    negated_parts(0)
                    for g in range(NG):
                        if g + 1 < NG:
                            maxima(g + 1)
                        dve.wait_ge(S["pv_mm"], STEPS * (g + 1))
                        if g >= 1:
                            dve.wait_ge(S["y_ready"], g)
                        nc.vector.tensor_copy(Y1, bank(6))
                        nc.vector.tensor_copy(Y2, bank(7)).then_inc(S["pv_copied"], 1)
                        if g + 1 < NG:
                            negated_parts(g + 1)
                        dve.wait_ge(S["den_mm"], g + 1)
                        nc.vector.reciprocal(R1, bank(6))
                        nc.vector.reciprocal(R2, bank(7)).then_inc(S["norm_ready"], 1)

            with nc.Block() as block:
                @block.sync
                def _(sp):
                    for e in range(NE):
                        sp.dma_start(ew1[e], w["ew1"][e].rearrange("(k p) n -> p k n", p=P)).then_inc(load_e[e], 16)
                        sp.dma_start(ew2[e], w["ew2"][e].rearrange("(k p) n -> p k n", p=P)).then_inc(load_e[e], 16)
                    sp.wait_ge(S["out_ready"], TT)
                    sp.dma_start(out[bass.ds(b, 1), :, :].rearrange("a (t p) n -> p (a t) n", p=P), mixed)\
                        .then_inc(S["stored"], 16)
                    sp.wait_ge(S["stored"], 16)

                @block.gpsimd
                def _(pool):
                    pool.wait_ge(S["xn_ready"], 3 * TT)
                    nc.gpsimd.tensor_tensor(x1[:], x1[:], xn[:], ALU.add).then_inc(S["res_added"], 1)

                @block.tensor
                def _(pe):
                    for t in range(TT):
                        for g in range(NG):
                            last = mm(bank(t)[:, 0:DM], YT[g][:, tok(t)], wp[:, g, :], g == 0, g == NG - 1)
                        last.then_inc(S["wp_mm"], 1)
                    to_columns(pe, xn2, 3 * TT, 4)
                    pe.wait_ge(S["xT_ready"], 6)
                    for t in range(TT):
                        for k in range(KM):
                            last = mm(bank(t)[:, 0:DM + NE], xT[:, k, tok(t)], abw[:, k, :], k == 0, k == KM - 1)
                        last.then_inc(S["ab_mm"], 1)

                    def hidden(e):
                        pe.wait_ge(load_e[e], 32)
                        for m in range(HT):
                            i = HT * e + m
                            if e == 0:
                                pe.wait_ge(S["abel_pre"], m + 1)
                            else:
                                pe.wait_ge(S["hid_ready"], i - HT + 1)
                            for k in range(KM):
                                last = mm(bank(m), ew1[e][:, k, m * P:(m + 1) * P], xT[:, k, :], k == 0, k == KM - 1)
                            last.then_inc(S["hid_mm"], 1)

                    def output(e):
                        pe.wait_ge(S["hid_ready"], HT * (e + 1))
                        if e == 1:
                            pe.wait_ge(S["moe_init"], 1)
                        if e >= 2:
                            pe.wait_ge(S["eo_added"], e - 1)
                        for t in range(TT):
                            for k in range(HT):
                                o = bank(4 + 2 * (e % 2) + t // 2)[:, (t % 2) * DM:(t % 2 + 1) * DM]
                                last = mm(o, hid[e % 2][:, k, tok(t)], ew2[e][:, k, :], k == 0, k == HT - 1)
                        last.then_inc(S["eo_mm"], 1)

                    hidden(0)
                    pe.wait_ge(S["sel_ready"], 1)
                    for t in range(TT):
                        last = nc.tensor.transpose(bank(6)[0:NE, tok(t)], sel[:, t, :], ident[:])
                    last.then_inc(S["wT_mm"], 1)
                    hidden(1)
                    pe.wait_ge(S["wT_ready"], 1)
                    for t in range(TT):
                        last = mm(bank(6 + t // 2)[:, (t % 2) * DM:(t % 2 + 1) * DM], selT[:, tok(t)], eb2[:], True, True)
                    last.then_inc(S["eb_mm"], 1)
                    for e in range(NE):
                        output(e)
                        if e + 2 < NE:
                            hidden(e + 2)
                    pe.wait_ge(S["eo_added"], NE)
                    for t in range(TT):
                        for k in range(KM):
                            last = nc.tensor.transpose(bank(k)[:, tok(t)], acc[:, t, k * P:(k + 1) * P], ident[:])
                    last.then_inc(S["moeT_mm"], 1)
                    pe.wait_ge(S["moeT_ready"], 2)
                    for t in range(TT):
                        for k in range(KM):
                            last = mm(bank(4 + t)[:, 0:DM], moeT[:, k, tok(t)], Wrot[:, k, :], k == 0, k == KM - 1)
                        last.then_inc(S["rot_mm"], 1)

                @block.scalar
                def _(act):
                    link = chain(act, S["act_chain5"])
                    inverse_root(act, link, 3)
                    inverse_root(act, link, 4)
                    act.wait_ge(S["xT_mm"], 6)
                    nc.scalar.activation(xT[:, 0, :], bank(4), ACT.Identity, bias=bet[:, 0:1], scale=gam[:, 0:1])\
                        .then_inc(S["xT_ready"], 1)
                    act.wait_ge(S["sel_d"], 2)
                    nc.scalar.activation(sel_ex[:], sel_ex[:], ACT.Exp).then_inc(S["sel_e"], 1)
                    nc.scalar.activation(sel_e2[:], sel_e2[:], ACT.Exp).then_inc(S["sel_e"], 1)
                    for e in range(NE):
                        for m in range(HT):
                            act.wait_ge(S["hid_mm"], HT * e + m + 1)
                            if e >= 2:
                                act.wait_ge(S["eo_mm"], e - 1)
                            nc.scalar.activation(hid[e % 2][:, m, :], bank(m), ACT.Gelu, bias=eb1[:, e, m:m + 1])\
                                .then_inc(S["hid_ready"], 1)
                        if e == 1:
                            nc.scalar.activation(ab[:, :, 0:DM], ab[:, :, 0:DM], ACT.Gelu).then_inc(S["abel_ready"], 1)
                    act.wait_ge(S["moeT_mm"], 1)
                    nc.scalar.activation(moeT[:, 0, :], bank(0), ACT.Copy).then_inc(S["moeT_ready"], 1)
                    act.wait_ge(S["gate_z"], 1)
                    nc.scalar.activation(gate[:, 1, :], gate[:, 0, :], ACT.Exp, scale=-1.0).then_inc(S["gate_e"], 1)

                @block.vector
                def _(dve):
                    link = chain(dve, S["dve_chain5"])
                    for t in range(TT):
                        dve.wait_ge(S["wp_mm"], t + 1)
                        link(nc.vector.tensor_tensor(x1[:, t, :], x1[:, t, :], bank(t)[:, 0:DM], ALU.add))
                    normalise(dve, link, x1, xn, 2, 3)
                    dve.wait_ge(S["xn_ready"], 3 * TT)
                    normalise(dve, link, xn, xn2, 3, 4)
                    dve.wait_ge(S["xT_mm"], 6)
                    nc.vector.tensor_scalar(xT[:, 1, :], bank(5), gam[:, 1:2], bet[:, 1:2], ALU.mult, ALU.add)\
                        .then_inc(S["xT_ready"], 1)
                    for t in range(TT):
                        dve.wait_ge(S["ab_mm"], t + 1)
                        nc.vector.tensor_tensor(ab[:, t, :], bank(t)[:, 0:DM + NE], abb[:], ALU.add)\
                            .then_inc(S["abel_pre"], 1)
                    dve.wait_ge(S["abel_pre"], TT)
                    lg = ab[:, :, DM:DM + NE]
                    for t in range(TT):
                        link(nc.vector.max(m8[:, t, :], ab[:, t, DM:DM + NE]))
                    m1, m2 = m8[:, :, 0:1], m8[:, :, 1:2]

                    def over(v):
                        return v.to_broadcast([P, TT, NE])

                    nc.vector.tensor_tensor(sel_ex[:], lg, over(m1), ALU.subtract).then_inc(S["sel_d"], 1)
                    nc.vector.tensor_tensor(sel_e2[:], m2, m1, ALU.subtract).then_inc(S["sel_d"], 1)
                    link(nc.vector.tensor_tensor(s_gt[:], lg, over(m2), ALU.is_gt))
                    link(nc.vector.tensor_tensor(s_eq[:], lg, over(m2), ALU.is_equal))
                    link(nc.vector.tensor_tensor(s_one[:], m1, m2, ALU.is_gt))
                    link(nc.vector.memset(s_zero[:], 0.0))
                    for t in range(TT):
                        link(nc.vector.tensor_tensor_scan(sel[:, t, :], s_eq[:, t, :], s_zero[:], 0.0,
                                                          ALU.add, ALU.add))
                    link(nc.vector.tensor_tensor(sel[:], sel[:], over(s_one[:]), ALU.add))
                    link(nc.vector.scalar_tensor_tensor(sel[:], sel[:], 2.0, s_eq[:], ALU.is_le, ALU.mult))
                    link(nc.vector.tensor_tensor(sel[:], sel[:], s_gt[:], ALU.add))
                    dve.wait_ge(S["sel_e"], 2)
                    link(nc.vector.tensor_scalar(s_den[:], sel_e2[:], 1.0, None, ALU.add))
                    link(nc.vector.reciprocal(s_den[:], s_den[:]))
                    link(nc.vector.tensor_tensor(sel[:], sel[:], sel_ex[:], ALU.mult))
                    nc.vector.tensor_tensor(sel[:], sel[:], over(s_den[:]), ALU.mult).then_inc(S["sel_ready"], 1)
                    dve.wait_ge(S["wT_mm"], 1)
                    nc.vector.tensor_copy(selT[:], bank(6)[0:NE]).then_inc(S["wT_ready"], 1)
                    dve.wait_ge(S["eb_mm"], 1)
                    nc.vector.tensor_copy(acc.rearrange("p t n -> p (t n)"),
                                          PS[:, 6:8, :].rearrange("p a n -> p (a n)")).then_inc(S["moe_init"], 1)
                    dve.wait_ge(S["moe_init"], 1)
                    dve.wait_ge(S["sel_ready"], 1)
                    for e in range(NE):
                        dve.wait_ge(S["eo_mm"], e + 1)
                        if e >= 1:
                            dve.wait_ge(S["eo_added"], e)
                        for t in range(TT):
                            o = bank(4 + 2 * (e % 2) + t // 2)[:, (t % 2) * DM:(t % 2 + 1) * DM]
                            last = nc.vector.scalar_tensor_tensor(acc[:, t, :], o, sel[:, t, e:e + 1], acc[:, t, :],
                                                                  ALU.mult, ALU.add)
                        last.then_inc(S["eo_added"], 1)
                    dve.wait_ge(S["moeT_mm"], 1)
                    nc.vector.tensor_copy(moeT[:, 1, :], bank(1)).then_inc(S["moeT_ready"], 1)
                    dve.wait_ge(S["abel_ready"], 1)
                    for t in range(TT):
                        link(nc.vector.tensor_tensor_reduce(out=mixed[:, t, :], in0=ab[:, t, 0:DM], in1=gcw[:, 0:DM],
                                                            scale=1.0, scalar=0.0, op0=ALU.mult, op1=ALU.add,
                                                            accum_out=gate[:, 2, t:t + 1]))
                    for t in range(TT):
                        dve.wait_ge(S["rot_mm"], t + 1)
                        link(nc.vector.tensor_tensor_reduce(out=mixed[:, t, :], in0=bank(4 + t)[:, 0:DM],
                                                            in1=gcw[:, DM:2 * DM], scale=1.0, scalar=0.0,
                                                            op0=ALU.mult, op1=ALU.add, accum_out=gate[:, 0, t:t + 1]))
                    link(nc.vector.tensor_tensor(gate[:, 0, :], gate[:, 0, :], gate[:, 2, :], ALU.add))
                    nc.vector.tensor_scalar(gate[:, 0, :], gate[:, 0, :], gcb[:, 0:1], -80.0, ALU.add, ALU.max)\
                        .then_inc(S["gate_z"], 1)
                    dve.wait_ge(S["gate_e"], 1)
                    link(nc.vector.tensor_scalar(gate[:, 1, :], gate[:, 1, :], 1.0, None, ALU.add))
                    link(nc.vector.reciprocal(gate[:, 1, :], gate[:, 1, :]))
                    dve.wait_ge(S["res_added"], 1)
                    for t in range(TT):
                        link(nc.vector.tensor_tensor(mixed[:, t, :], bank(4 + t)[:, 0:DM], ab[:, t, 0:DM], ALU.subtract))
                        link(nc.vector.scalar_tensor_tensor(mixed[:, t, :], mixed[:, t, :], gate[:, 1, t:t + 1],
                                                            ab[:, t, 0:DM], ALU.mult, ALU.add))
                        nc.vector.tensor_tensor(mixed[:, t, :], mixed[:, t, :], x1[:, t, :], ALU.add)\
                            .then_inc(S["out_ready"], 1)
            reset()


def kernel(**inputs):
    import numpy as np
    import concourse.bacc as bacc
    from concourse.bass_utils import run_bass_kernel_spmd

    attn = {n: np.asarray(inputs["L0_attn_" + n]) for n in
            ("in_proj_w", "conv_w", "conv_b", "x_proj_w", "dt_proj_w", "dt_proj_b", "A_log", "D", "out_proj_w")}
    arrays = {
        "in_proj_wT": attn["in_proj_w"].T, "conv_w": attn["conv_w"][:, 0, :], "conv_b": attn["conv_b"],
        "x_proj_wT": attn["x_proj_w"].T, "dt_proj_wT": attn["dt_proj_w"].T, "dt_proj_b": attn["dt_proj_b"],
        "A_log": attn["A_log"], "D": attn["D"], "out_proj_wT": attn["out_proj_w"].T,
    }
    for n in ("Wk", "bk", "Wq", "bq", "Wv", "bv", "Wck", "bck", "Wcq", "bcq", "Wcv", "bcv", "Wp", "bp"):
        arrays[n] = np.asarray(inputs["L0_xattn_" + n])
    for n in ("ln_gamma", "ln_beta", "abel_w", "abel_b", "moe_gate_w", "moe_gate_b", "ew1", "eb1", "ew2", "eb2",
              "gens", "gc_w", "gc_b"):
        arrays[n] = np.asarray(inputs["L0_ffn_" + n])
    for n in ("conv_b", "dt_proj_b", "D", "bq", "bk", "bcq", "bck", "ln_gamma", "ln_beta"):
        arrays[n] = arrays[n].reshape(-1, P).T
    arrays["eb1"] = arrays["eb1"].reshape(NE, HT, P).transpose(2, 0, 1)
    arrays["x"] = np.asarray(inputs["x"])
    arrays["ctx_t"] = np.asarray(inputs["ctx_512"]).transpose(0, 2, 1)

    nc = bacc.Bacc("TRN2", target_bir_lowering=False, num_devices=1)
    feed, aps = {}, {}
    for name, a in arrays.items():
        a = np.ascontiguousarray(a)
        feed[f"in_{name}"] = a
        aps[name] = nc.dram_tensor(f"in_{name}", a.shape, mybir.dt.from_np(a.dtype), kind="ExternalInput").ap()
    out = nc.dram_tensor("out", (NB, T, DM), F32, kind="ExternalOutput").ap()
    decoder(nc, aps, aps["x"], aps["ctx_t"], out)
    r = run_bass_kernel_spmd(nc, [feed], core_ids=[0])
    return r.results[0]["out"]
```

```python
import concourse.bass as bass
from concourse import mybir
from contextlib import ExitStack
from math import factorial

F32 = mybir.dt.float32
BF16 = mybir.dt.bfloat16
I32 = mybir.dt.int32
ALU = mybir.AluOpType
ACT = mybir.ActivationFunctionType
AXX = mybir.AxisListType.X

P = 128
NB, T, DM = 4, 512, 256
TC, CC = 1024, 128
TT = T // P
KM = DM // P
DI, NS, DCONV, RK = 512, 16, 4, 64
DT = DI // P
H, HD = 16, 16
HG = 4
NG = H // HG
VW = 32
SK = 6 * HD
SR = SK + 3
NPAR = 3
NPT = 9
NE, HID = 8, 512
HT = HID // P
NGEN, SQUARINGS = 3, 6
EPS = 1e-5
MASKED = -1e30
Q_PART = [0, 0, 0, 1, 1, 2]
K_PART = [0, 1, 2, 0, 1, 0]


def decoder(nc, w, x_in, ctx_t, out):
    qkv_dram = nc.dram_tensor("stack_parts", (4, 3, H, HD, TC), BF16).ap()
    with ExitStack() as ctx:
        sems = []

        def sb(name, shape, dt=F32):
            return ctx.enter_context(nc.sbuf_tensor(name, shape, dt))

        def sem(name):
            s = ctx.enter_context(nc.semaphore(name))
            sems.append(s)
            return s

        PS = ctx.enter_context(nc.psum_tensor("PS", [P, 8, 512], F32))

        def bank(i):
            return PS[:, i, :]

        in_w = sb("in_w", [P, KM, 2 * DI])
        conv_w = sb("conv_w", [P, DT, DCONV])
        conv_b = sb("conv_b", [P, DT])
        xproj_w = sb("xproj_w", [P, DT, RK + 2 * NS])
        dt_w = sb("dt_w", [RK, DI])
        dt_b = sb("dt_b", [P, DT])
        A_neg = sb("A_neg", [P, DT, NS])
        D_skip = sb("D_skip", [P, DT])
        out_w = sb("out_w", [P, DT, DM])
        wq = sb("wq", [P, KM, DM])
        wk = sb("wk", [P, KM, DM])
        wv = sb("wv", [P, KM, DM])
        wcq = sb("wcq", [P, KM, DM])
        wck = sb("wck", [P, DM])
        wcv = sb("wcv", [P, DM])
        bqk = sb("bqk", [P, 4, KM])
        bv = sb("bv", [P, DM])
        bcv = sb("bcv", [P, DM])
        wp = sb("wp", [P, NG, DM])
        bp = sb("bp", [P, DM])
        gam = sb("gam", [P, KM])
        bet = sb("bet", [P, KM])
        abw = sb("abw", [P, KM, DM + NE])
        abb = sb("abb", [P, DM + NE])
        eb1 = sb("eb1", [P, NE, HT])
        eb2 = sb("eb2", [NE, DM])
        gcw = sb("gcw", [P, 2 * DM])
        gcb = sb("gcb", [P, 1])
        Wrot = sb("Wrot", [P, KM, DM])
        ident = sb("ident", [P, P])
        identb = sb("identb", [P, P], BF16)
        mask_qk = sb("mask_qk", [P, P], BF16)
        mask_kq = sb("mask_kq", [P, P], BF16)
        den_sel = sb("den_sel", [P, P])
        bc_sel = sb("bc_sel", [6 * NS, 2 * NS, P], BF16)
        eps_t = sb("eps_t", [P, 1])
        x_sb = sb("x_sb", [P, TT, DM])
        x1 = sb("x1", [P, TT, DM])
        xn = sb("xn", [P, TT, DM])
        xT = sb("xT", [P, KM, T])
        ctxT = sb("ctxT", [P, TC])
        stats = sb("stats", [P, TT, 6])
        mv = sb("mv", [P, TT, 2])
        rs = sb("rs", [P, 4, TT])
        dtin = sb("dtin", [RK, T])
        bc3 = sb("bc3", [6 * NS, T], BF16)
        bcr = sb("bcr", [2 * NS, 2, T])
        maxs = sb("maxs", [P, 2, TT, 2 * HG])
        mparts = sb("mparts", [HG, 2, 3, T], BF16)
        den_sb = xn[:].rearrange("p (a t) n -> p a (t n)", a=2)
        mrest = sb("mrest", [HG, T])
        m8 = sb("m8", [P, TT, 8])
        sel = sb("sel", [P, TT, NE])
        sel_ex = sb("sel_ex", [P, TT, NE])
        sel_e2 = sb("sel_e2", [P, TT, 1])
        s_gt = sb("s_gt", [P, TT, NE])
        s_eq = sb("s_eq", [P, TT, NE])
        s_one = sb("s_one", [P, TT, 1])
        s_zero = sb("s_zero", [P, NE])
        s_den = sb("s_den", [P, TT, 1])
        selT = sb("selT", [NE, T])
        gate = sb("gate", [P, 3, TT])
        table_at = sb("table_at", [P, 1])
        NAR = 29696
        arena = sb("arena", [P, NAR])
        used = [0]

        def ar(n, dt=F32):
            words = n if dt == F32 else n // 2
            v = arena[:, used[0]:used[0] + words]
            used[0] += words
            assert used[0] <= NAR, used[0]
            return v if dt == F32 else v.bitcast(dt)

        def ar_start(at=0):
            used[0] = at

        def mm(o, l, r, start, stop):
            return nc.tensor.matmul(o, l, r, start=start, stop=stop)

        def reset():
            numbers = sorted(s.num for s in sems)
            assert numbers == list(range(numbers[0], numbers[-1] + 1))
            nc.gpsimd.sem_clear(range(numbers[0], numbers[-1] + 1))
            nc.all_engine_barrier()

        load_w = sem("load_w")
        load_a = sem("load_a")
        load_gen = sem("load_gen")
        const_ready = sem("const_ready")
        id_ready = sem("id_ready")
        exp_mm = sem("exp_mm")
        exp_ev = sem("exp_ev")
        a_ready = sem("a_ready")
        pool_chain = sem("pool_chain")
        dve_chain = sem("dve_chain")
        act_chain = sem("act_chain")

        def chain(eng, s):
            count = [0]

            def link(ins):
                count[0] += 1
                ins.then_inc(s, 1)
                eng.wait_ge(s, count[0])
            link.sem, link.count = s, count
            return link

        ar_start()
        G = [{n: ar(KM * DM).rearrange("p (k n) -> p k n", k=KM)
              for n in ("A", "T", "A2", "A3", "X")} for _ in range(NGEN)]
        Iw = ar(KM * DM).rearrange("p (k n) -> p k n", k=KM)
        A_raw = ar(DT * NS).rearrange("p (k n) -> p k n", k=DT)
        coef = [1.0 / factorial(i) for i in range(13)]
        N_STEPS = 4 + 1 + 3 + 2 * SQUARINGS
        with nc.Block() as block:
            @block.sync
            def _(sp):
                for g in range(NGEN):
                    sp.dma_start(G[g]["A"], w["gens"][g].rearrange("(k p) n -> p k n", p=P)).then_inc(load_gen, 16)
                sp.dma_start(A_raw, w["A_log"].rearrange("(k p) n -> p k n", p=P)).then_inc(load_a, 16)
                n = 0
                loads = [
                    (in_w[:], w["in_proj_wT"].rearrange("(k p) n -> p k n", p=P)),
                    (conv_w[:], w["conv_w"].rearrange("(k p) n -> p k n", p=P)),
                    (conv_b[:], w["conv_b"]),
                    (xproj_w[:], w["x_proj_wT"].rearrange("(k p) n -> p k n", p=P)),
                    (dt_w[:], w["dt_proj_wT"]),
                    (dt_b[:], w["dt_proj_b"]),
                    (D_skip[:], w["D"]),
                    (out_w[:], w["out_proj_wT"].rearrange("(k p) n -> p k n", p=P)),
                    (wq[:], w["Wq"].rearrange("(k p) n -> p k n", p=P)),
                    (wk[:], w["Wk"].rearrange("(k p) n -> p k n", p=P)),
                    (wv[:], w["Wv"].rearrange("(k p) n -> p k n", p=P)),
                    (wcq[:], w["Wcq"].rearrange("(k p) n -> p k n", p=P)),
                    (wck[:], w["Wck"]),
                    (wcv[:], w["Wcv"]),
                    (bqk[:, 0, :], w["bq"]),
                    (bqk[:, 1, :], w["bk"]),
                    (bqk[:, 2, :], w["bcq"]),
                    (bqk[:, 3, :], w["bck"]),
                    (bv[:], w["bv"].partition_broadcast(P)),
                    (bcv[:], w["bcv"].partition_broadcast(P)),
                    (bp[:], w["bp"].partition_broadcast(P)),
                    (gam[:], w["ln_gamma"]),
                    (bet[:], w["ln_beta"]),
                    (abw[:, :, 0:DM], w["abel_w"].rearrange("(k p) n -> p k n", p=P)),
                    (abw[:, :, DM:DM + NE], w["moe_gate_w"].rearrange("(k p) n -> p k n", p=P)),
                    (abb[:, 0:DM], w["abel_b"].partition_broadcast(P)),
                    (abb[:, DM:DM + NE], w["moe_gate_b"].partition_broadcast(P)),
                    (eb1[:], w["eb1"]),
                    (eb2[:], w["eb2"]),
                    (gcw[:], w["gc_w"].rearrange("n o -> (n o)").partition_broadcast(P)),
                    (gcb[:], w["gc_b"].partition_broadcast(P)),
                ]
                for o, i in loads:
                    sp.dma_start(o, i).then_inc(load_w, 16)
                    n += 16
                sp.wait_ge(const_ready, 1)
                for g in range(NG):
                    for j in range(HG):
                        r = (g * HG + j) * HD
                        sp.dma_start(wp[32 * j:32 * j + HD, g, :], w["Wp"][r:r + HD, :]).then_inc(load_w, 16)
                        n += 16
                sp.wait_ge(load_w, n)

            @block.gpsimd
            def _(pool):
                link = chain(pool, pool_chain)
                nc.gpsimd.memset(ident[:], 0.0).then_inc(id_ready, 1)
                pool.wait_ge(id_ready, 1)
                nc.gpsimd.affine_select(out=ident[:], in_=ident[:], compare_op=ALU.not_equal, fill=1.0, base=0,
                                        pattern=[[-1, P]], channel_multiplier=1).then_inc(id_ready, 1)
                nc.gpsimd.memset(wp[:], 0.0).then_inc(const_ready, 1)
                link(nc.gpsimd.memset(Iw, 0.0))
                for k in range(KM):
                    link(nc.gpsimd.affine_select(out=Iw[:, k, :], in_=Iw[:, k, :], compare_op=ALU.not_equal, fill=1.0,
                                                 base=k * P, pattern=[[-1, DM]], channel_multiplier=1))
                pool.wait_ge(id_ready, 2)
                link(nc.gpsimd.tensor_copy(identb[:], ident[:]))
                link(nc.gpsimd.memset(mask_qk[:], 0.0))
                link(nc.gpsimd.memset(mask_kq[:], 0.0))
                link(nc.gpsimd.affine_select(out=mask_qk[:], in_=mask_qk[:], compare_op=ALU.is_ge, fill=MASKED, base=0,
                                             pattern=[[-1, P]], channel_multiplier=1))
                link(nc.gpsimd.affine_select(out=mask_kq[:], in_=mask_kq[:], compare_op=ALU.is_ge, fill=MASKED, base=0,
                                             pattern=[[1, P]], channel_multiplier=-1))
                link(nc.gpsimd.memset(den_sel[:], 0.0))
                v = den_sel[:].rearrange("p (a c) -> p a c", c=32)
                link(nc.gpsimd.affine_select(out=v, in_=v, compare_op=ALU.not_equal, fill=1.0, base=-HD,
                                             pattern=[[-32, 4], [0, 32]], channel_multiplier=1))
                link(nc.gpsimd.memset(bc_sel[:], 0.0))
                for part in range(3):
                    link(nc.gpsimd.affine_select(out=bc_sel[:], in_=bc_sel[:], compare_op=ALU.not_equal, fill=1.0,
                                                 base=-32 * part, pattern=[[-1, 2 * NS], [0, P]], channel_multiplier=1))
                nc.gpsimd.memset(eps_t[:], EPS).then_inc(const_ready, 1)

            @block.scalar
            def _(act):
                act.wait_ge(load_a, 16)
                nc.scalar.activation(A_neg[:], A_raw, ACT.Exp).then_inc(a_ready, 1)

            @block.tensor
            def _(pe):
                step = [0]

                def ready(g):
                    pe.wait_ge(exp_ev, NGEN * step[0] + g + 1)

                def o3(g):
                    return bank(g).rearrange("p (k n) -> p k n", k=KM)

                def product(lT, r):
                    for g in range(NGEN):
                        ready(g)
                        for m in range(KM):
                            for k in range(KM):
                                last = mm(o3(g)[:, m, :], G[g][lT][:, k, m * P:(m + 1) * P], G[g][r][:, k, :],
                                          k == 0, k == KM - 1)
                        last.then_inc(exp_mm, 1)
                    step[0] += 1

                def transposed(s):
                    for g in range(NGEN):
                        ready(g)
                        for m in range(KM):
                            for k in range(KM):
                                last = nc.tensor.transpose(o3(g)[:, m, k * P:(k + 1) * P],
                                                           G[g][s][:, k, m * P:(m + 1) * P], ident[:])
                        last.then_inc(exp_mm, 1)
                    step[0] += 1

                pe.wait_ge(id_ready, 2)
                transposed("A")
                product("T", "A")
                product("T", "A2")
                transposed("A3")
                for _ in range(3):
                    product("T", "X")
                for s in range(SQUARINGS):
                    transposed("X")
                    if s < SQUARINGS - 1:
                        product("T", "X")
                for g in range(NGEN):
                    ready(g)
                    lT, r = ("T", "X") if g == NGEN - 1 else ("X", "T")
                    for m in range(KM):
                        for k in range(KM):
                            last = mm(o3(g)[:, m, :], G[g][lT][:, k, m * P:(m + 1) * P], G[g][r][:, k, :],
                                      k == 0, k == KM - 1)
                    last.then_inc(exp_mm, 1)
                step[0] += 1
                for i, (g, r) in enumerate(((1, G[2]["X"]), (0, G[2]["T"]))):
                    pe.wait_ge(exp_ev, NGEN * (step[0] + 1) + i)
                    for m in range(KM):
                        for k in range(KM):
                            last = mm(o3(i)[:, m, :], G[g]["X"][:, k, m * P:(m + 1) * P], r[:, k, :],
                                      k == 0, k == KM - 1)
                    last.then_inc(exp_mm, 1)

            @block.vector
            def _(dve):
                link = chain(dve, dve_chain)
                done = [0]

                def o3(g):
                    return bank(g).rearrange("p (k n) -> p k n", k=KM)

                def product_ready():
                    done[0] += 1
                    dve.wait_ge(exp_mm, done[0])

                def evac(dst):
                    for g in range(NGEN):
                        product_ready()
                        nc.vector.tensor_copy(G[g][dst], o3(g)).then_inc(exp_ev, 1)

                for g in range(NGEN):
                    dve.wait_ge(load_gen, 16 * (g + 1))
                dve.wait_ge(a_ready, 1)
                link(nc.vector.tensor_scalar(A_neg[:], A_neg[:], -1.0, None, ALU.mult))
                for g in range(NGEN):
                    nc.vector.tensor_scalar(G[g]["A"], G[g]["A"], 2.0 ** -SQUARINGS, None,
                                            ALU.mult).then_inc(exp_ev, 1)
                evac("T")
                evac("A2")
                dve.wait_ge(pool_chain, 3)
                for g in range(NGEN):
                    product_ready()
                    nc.vector.tensor_copy(G[g]["A3"], o3(g)).then_inc(exp_ev, 1)
                for g in range(NGEN):
                    X, A, A2, A3 = (G[g][n] for n in ("X", "A", "A2", "A3"))
                    product_ready()
                    link(nc.vector.tensor_copy(G[g]["T"], o3(g)))
                    link(nc.vector.tensor_scalar(X, A3, coef[12], None, ALU.mult))
                    link(nc.vector.scalar_tensor_tensor(X, A2, coef[11], X, ALU.mult, ALU.add))
                    link(nc.vector.scalar_tensor_tensor(X, A, coef[10], X, ALU.mult, ALU.add))
                    nc.vector.scalar_tensor_tensor(X, Iw, coef[9], X, ALU.mult, ALU.add).then_inc(exp_ev, 1)
                for i in (6, 3, 0):
                    for g in range(NGEN):
                        X, A, A2 = (G[g][n] for n in ("X", "A", "A2"))
                        product_ready()
                        link(nc.vector.scalar_tensor_tensor(X, A2, coef[i + 2], o3(g), ALU.mult, ALU.add))
                        link(nc.vector.scalar_tensor_tensor(X, A, coef[i + 1], X, ALU.mult, ALU.add))
                        nc.vector.scalar_tensor_tensor(X, Iw, coef[i], X, ALU.mult, ALU.add).then_inc(exp_ev, 1)
                for s in range(SQUARINGS):
                    evac("T")
                    evac("X")
                product_ready()
                nc.vector.tensor_copy(G[2]["T"], o3(0)).then_inc(exp_ev, 1)
                product_ready()
                nc.vector.tensor_copy(Wrot[:], o3(1)).then_inc(exp_ev, 1)
        reset()

        names = """load_x load_ctx xn_ready xT_mm xT_ready inproj_mm xp_ready xc_ready xs_ready z_ready
            xdbl_mm dtin_ready bc_hi bc3_ready dt_mm abs_done sp_ready
            bn_mm cn_mm bn_copied b0_ready b_ready a_done h_done g_done y_mm g_last y_last
            gated outproj_mm bp_added qkv_mm hi_f_ready mid_ready parts_ready v_mm v_init v_ready
            ones_ready max_mm max_done mt_mm half_ready mt_read mparts_ready ring_mm ring_read pv_mm pv_copied norm_ready
            y_ready wp_mm res_added hid_mm hid_ready eo_mm eo_added ab_mm abel_pre abel_ready sel_d sel_e sel_ready
            wT_mm wT_ready eb_mm moe_init moeT_mm moeT_ready rot_mm gate_z gate_e out_ready stored dve_chain1 act_chain1 dve_chain2 dve_chain3 act_chain3
            pool_chain4 dve_chain4 den_ready act_chain5 dve_chain5""".split()
        S = {n: sem(n) for n in names}
        parts_stored = [sem(f"parts_stored{i}") for i in range(NPT)]
        stack_in = [sem(f"stack_in{g}") for g in range(NG)]
        max_rows = [[sem(f"max_rows{g}_{side}") for side in ("context", "causal")] for g in range(NG)]
        load_e = [sem(f"load_e{e}") for e in range(NE)]

        def four(n=T):
            return ar(DT * n).rearrange("p (k n) -> p k n", k=DT)

        def stack(n):
            return ar(HG * n, BF16).rearrange("p (h n) -> p h n", h=HG)

        ar_start()
        delta, u, xs, zs = four(), four(), four(), four()
        scan_at = used[0]
        xp, xc, tmp = four(T + 4), four(), four()
        ar_start(scan_at)
        a_sb = [four(), four()]
        b_sb = [four(), four()]
        g_sb = [four(), four()]
        h_sb = [four(), four()]
        Bn = [ar(T), ar(T)]
        ar_start(scan_at)
        f_sb = [ar(T), ar(T)]
        r_sb = [ar(T), ar(T)]
        pt = [ar(3 * T, BF16).rearrange("p (k n) -> p k n", k=3) for _ in range(4)]
        pre_at = used[0]
        V = ar(TT * H * VW).rearrange("p (t h d) -> p t h d", t=TT, h=H)
        VC = ar(2 * TT * H * VW).rearrange("p (t h d) -> p t h d", t=2 * TT, h=H)
        KC = [stack(TC) for _ in range(NPAR)]
        NPR = 8
        probs_at = used[0]
        probs = [ar(T) for _ in range(NPR)]
        ar_start(probs_at + NPR // 2 * T)
        running = ar(TT * T).rearrange("p (t n) -> p t n", t=TT)
        ar_start(probs_at)
        pt += [ar(3 * T, BF16).rearrange("p (k n) -> p k n", k=3) for _ in range(NPT - 4)]
        ar_start()
        Q = [stack(T) for _ in range(NPAR)]
        K = [stack(T) for _ in range(NPAR)]
        C = [stack(T) for _ in range(NPAR)]
        YT = [ar(T) for _ in range(NG)]
        yt_end = used[0]
        Y1, Y2, R1, R2 = ar(T), ar(T), ar(T), ar(T)
        assert used[0] <= pre_at
        ar_start()
        hid = [four(), four()]
        ab = ar(TT * (DM + NE)).rearrange("p (t n) -> p t n", t=TT)
        acc = ar(TT * DM).rearrange("p (t n) -> p t n", t=TT)
        moeT = ar(KM * T).rearrange("p (k n) -> p k n", k=KM)
        assert used[0] <= NPAR * 3 * HG * T // 2
        ar_start(yt_end)
        xn2 = ar(TT * DM).rearrange("p (t n) -> p t n", t=TT)
        mixed = ar(TT * DM).rearrange("p (t n) -> p t n", t=TT)
        assert used[0] <= pre_at
        diff = hid[0].rearrange("p k n -> p (k n)")[:, 0:TT * DM].rearrange("p (t n) -> p t n", t=TT)
        ar_start(pre_at)
        ew1 = [ar(KM * HID).rearrange("p (k n) -> p k n", k=KM) for _ in range(NE)]
        ew2 = [ar(HT * DM).rearrange("p (k n) -> p k n", k=HT) for _ in range(NE)]

        def normalise(dve, link, src, dst, source=None):
            for t in range(TT):
                if source:
                    source(t)
                nc.vector.bn_stats(out=stats[:, t, :], in_=src[:, t, :]).then_inc(link.sem, 1)
                link.count[0] += 1
            dve.wait_ge(link.sem, link.count[0])
            for t in range(TT):
                nc.vector.bn_aggr(out=mv[:, t, :], in_=stats[:, t, :]).then_inc(link.sem, 1)
            link.count[0] += TT
            dve.wait_ge(link.sem, link.count[0])
            v, h, y, z = (rs[:, i, :] for i in range(4))
            nc.vector.tensor_scalar(h, mv[:, :, 1], EPS, -0.5, ALU.add, ALU.mult).then_inc(link.sem, 1)
            link.count[0] += 1
            link(nc.vector.tensor_scalar(v, mv[:, :, 1], EPS, None, ALU.add))
            link(nc.vector.tensor_scalar(z.bitcast(I32), v.bitcast(I32), 1, None, ALU.logical_shift_right))
            link(nc.vector.tensor_scalar(y.bitcast(I32), z.bitcast(I32), -1.0, float(0x5f3759df), ALU.mult, ALU.add))
            for _ in range(3):
                link(nc.vector.tensor_tensor(z, y, y, ALU.mult))
                link(nc.vector.tensor_tensor(z, z, h, ALU.mult))
                link(nc.vector.scalar_tensor_tensor(y, z, 1.5, y, ALU.add, ALU.mult))
            for t in range(TT):
                nc.vector.tensor_scalar(dst[:, t, :], src[:, t, :], mv[:, t, 0:1], rs[:, 2, t:t + 1],
                                        ALU.subtract, ALU.mult).then_inc(S["xn_ready"], 1)

        def to_columns(pe, src, n, b0):
            for t in range(TT):
                pe.wait_ge(S["xn_ready"], n + t + 1)
                for k in range(KM):
                    last = nc.tensor.transpose(bank(b0 + k)[:, t * P:(t + 1) * P], src[:, t, k * P:(k + 1) * P],
                                               ident[:])
                    if t == TT - 1:
                        last.then_inc(S["xT_mm"], 1)

        def load_stack(sp, g, i):
            x, dst, parts, n = ((2, C, Q_PART, T), (3, KC, K_PART, TC), (0, Q, Q_PART, T), (1, K, K_PART, T))[i]
            heads = slice(g * HG, (g + 1) * HG)
            for j, part in enumerate(parts):
                sp.dma_start(dst[g % NPAR][j * HD:(j + 1) * HD],
                             qkv_dram[x, part, heads, :, 0:n].rearrange("h d t -> d h t"))\
                    .then_inc(stack_in[g], 16)

        def load_stacks(sp, g):
            for i in range(4):
                load_stack(sp, g, i)

        def tok(t):
            return slice(t * P, (t + 1) * P)

        with nc.Fori(0, NB) as b:
            with nc.Block() as block:
                @block.sync
                def _(sp):
                    sp.dma_start(x_sb[:], x_in[bass.ds(b, 1), :, :].rearrange("a (t p) n -> p (a t) n", p=P))\
                        .then_inc(S["load_x"], 16)
                    sp.dma_start(ctxT[:], ctx_t[bass.ds(b, 1), :, :].rearrange("a c n -> (a c) n"))\
                        .then_inc(S["load_ctx"], 16)

                @block.tensor
                def _(pe):
                    to_columns(pe, xn, 0, 0)
                    pe.wait_ge(S["xT_ready"], 2)
                    for m in range(2 * DT):
                        if m == 6:
                            pass
                        for k in range(KM):
                            last = mm(bank((2 + m) % 8), in_w[:, k, m * P:(m + 1) * P], xT[:, k, :], k == 0, k == KM - 1)
                        last.then_inc(S["inproj_mm"], 1)
                    for k in range(DT):
                        pe.wait_ge(S["xs_ready"], k + 1)
                        last = mm(bank(2)[0:RK + 2 * NS], xproj_w[:, k, :], xs[:, k, :], k == 0, k == DT - 1)
                    last.then_inc(S["xdbl_mm"], 1)
                    pe.wait_ge(S["dtin_ready"], 1)
                    for m in range(DT):
                        mm(bank(4 + m), dt_w[:, m * P:(m + 1) * P], dtin[:], True, True).then_inc(S["dt_mm"], 1)

                @block.scalar
                def _(act):
                    link = chain(act, S["act_chain1"])
                    act.wait_ge(S["xT_mm"], 2)
                    nc.scalar.activation(xT[:, 0, :], bank(0), ACT.Copy).then_inc(S["xT_ready"], 1)
                    for m in range(DT):
                        act.wait_ge(S["inproj_mm"], m + 1)
                        nc.scalar.activation(xp[:, m, 3:3 + T], bank(2 + m), ACT.Copy).then_inc(S["xp_ready"], 1)
                    for m in range(DT):
                        act.wait_ge(S["xc_ready"], m + 1)
                        nc.scalar.activation(xs[:, m, :], xc[:, m, :], ACT.Silu).then_inc(S["xs_ready"], 1)
                        act.wait_ge(S["inproj_mm"], DT + m + 1)
                        nc.scalar.activation(zs[:, m, :], bank((6 + m) % 8), ACT.Silu).then_inc(S["z_ready"], 1)
                    nc.scalar.activation(table_at[:], dt_b[:, 0:1], ACT.Exp)
                    act.wait_ge(S["xdbl_mm"], 1)
                    nc.scalar.activation(dtin[:], bank(2)[0:RK], ACT.Copy).then_inc(S["dtin_ready"], 1)
                    nc.scalar.activation(bc3[0:2 * NS], bank(2)[RK:RK + 2 * NS], ACT.Copy).then_inc(S["bc_hi"], 1)
                    for m in range(DT):
                        act.wait_ge(S["dt_mm"], m + 1)
                        nc.scalar.activation(tmp[:, m, :], bank(4 + m), ACT.Abs, bias=dt_b[:, m:m + 1])\
                            .then_inc(S["abs_done"], 1)
                        act.wait_ge(S["abs_done"], m + 1)
                        ins = nc.scalar.activation(tmp[:, m, :], tmp[:, m, :], ACT.Exp, scale=-1.0)
                    link(ins)
                    for m in range(DT):
                        nc.scalar.activation(tmp[:, m, :], tmp[:, m, :], ACT.Ln, bias=1.0).then_inc(S["sp_ready"], 1)
                    link(nc.scalar.activation(table_at[:], dt_b[:, 0:1], ACT.Exp))

                @block.vector
                def _(dve):
                    link = chain(dve, S["dve_chain1"])
                    dve.wait_ge(S["load_x"], 16)
                    normalise(dve, link, x_sb, xn)
                    link(nc.vector.memset(xp[:, :, 0:3], 0.0))
                    dve.wait_ge(S["xT_mm"], 2)
                    nc.vector.tensor_copy(xT[:, 1, :], bank(1)).then_inc(S["xT_ready"], 1)
                    for m in range(DT):
                        dve.wait_ge(S["xp_ready"], m + 1)
                        link(nc.vector.tensor_scalar(xc[:, m, :], xp[:, m, 0:T], conv_w[:, m, 0:1], conv_b[:, m:m + 1],
                                                     ALU.mult, ALU.add))
                        for j in range(1, DCONV):
                            ins = nc.vector.scalar_tensor_tensor(xc[:, m, :], xp[:, m, j:j + T], conv_w[:, m, j:j + 1],
                                                                 xc[:, m, :], ALU.mult, ALU.add)
                            if j < DCONV - 1:
                                link(ins)
                        ins.then_inc(S["xc_ready"], 1)
                    dve.wait_ge(S["bc_hi"], 1)
                    link(nc.vector.tensor_tensor(bcr[:, 0, :], bank(2)[RK:RK + 2 * NS], bc3[0:2 * NS], ALU.subtract))
                    nc.vector.tensor_copy(bc3[2 * NS:4 * NS], bcr[:, 0, :]).then_inc(S["bc3_ready"], 1)
                    mid = bcr[:, 1, :].bitcast(BF16)[:, 0:T]
                    link(nc.vector.tensor_copy(mid, bcr[:, 0, :]))
                    nc.vector.tensor_tensor(bc3[4 * NS:6 * NS], bcr[:, 0, :], mid, ALU.subtract)\
                        .then_inc(S["bc3_ready"], 1)
                    for m in range(DT):
                        dve.wait_ge(S["abs_done"], m + 1)
                        last = nc.vector.tensor_scalar(delta[:, m, :], bank(4 + m), dt_b[:, m:m + 1], 0.0, ALU.add,
                                                       ALU.max)
                    link(last)
                    for m in range(DT):
                        dve.wait_ge(S["sp_ready"], m + 1)
                        link(nc.vector.tensor_tensor(delta[:, m, :], delta[:, m, :], tmp[:, m, :], ALU.add))
                        last = nc.vector.tensor_tensor(u[:, m, :], delta[:, m, :], xs[:, m, :], ALU.mult)
                    link(last)

            with nc.Block() as block:
                @block.tensor
                def _(pe):
                    def sum_states(n):
                        for k in range(DT):
                            if n == NS - 1:
                                pe.wait_ge(S["g_last"], k + 1)
                            last = mm(bank(k), ident[:], g_sb[n % 2][:, k, :], n == 0, n == NS - 1)
                            if n == NS - 1:
                                last.then_inc(S["y_last"], 1)
                        if n < NS - 1:
                            last.then_inc(S["y_mm"], 1)

                    def rows(n, first, to, done):
                        mm(bank(to + n % 2), bc_sel[:, first + n, :], bc3[:], True, True).then_inc(S[done], 1)

                    for n in range(2):
                        rows(n, 0, 4, "bn_mm")
                        rows(n, NS, 6, "cn_mm")
                    pe.wait_ge(S["bn_copied"], 1)
                    rows(2, 0, 4, "bn_mm")
                    for n in range(NS):
                        if n + 3 < NS:
                            pe.wait_ge(S["bn_copied"], n + 2)
                            rows(n + 3, 0, 4, "bn_mm")
                        if n < NS - 1:
                            pe.wait_ge(S["g_done"], n + 1)
                        if n + 2 < NS:
                            rows(n + 2, NS, 6, "cn_mm")
                        sum_states(n)

                @block.scalar
                def _(act):
                    for n in range(NS):
                        act.wait_ge(S["bn_mm"], n + 1)
                        if n == 2:
                            act.wait_ge(S["b0_ready"], 1)
                        if n > 2:
                            act.wait_ge(S["b_ready"], n - 2)
                        nc.scalar.activation(Bn[n % 2], bank(4 + n % 2), ACT.Copy).then_inc(S["bn_copied"], 1)
                        if n >= 2:
                            act.wait_ge(S["h_done"], n - 1)
                        for k in range(DT):
                            last = nc.scalar.activation(a_sb[n % 2][:, k, 1:T], delta[:, k, 1:T], ACT.Exp,
                                                        scale=A_neg[:, k, n:n + 1])
                        last.then_inc(S["a_done"], 1)

                @block.gpsimd
                def _(pool):
                    for n in range(1, NS):
                        pool.wait_ge(S["bn_copied"], n + 1)
                        if n >= 2:
                            pool.wait_ge(S["h_done"], n - 1)
                        nc.gpsimd.tensor_tensor(b_sb[n % 2], u, Bn[n % 2].unsqueeze(1).to_broadcast([P, DT, T]),
                                                ALU.mult).then_inc(S["b_ready"], 1)

                @block.vector
                def _(dve):
                    link = chain(dve, S["dve_chain2"])
                    flat = "p k n -> p (k n)"
                    for i in range(2):
                        link(nc.vector.memset(a_sb[i][:, :, 0:1], 0.0))
                    for n in range(NS):
                        if n == 0:
                            dve.wait_ge(S["bn_copied"], 1)
                            nc.vector.tensor_tensor(b_sb[0], u, Bn[0].unsqueeze(1).to_broadcast([P, DT, T]),
                                                    ALU.mult).then_inc(S["b0_ready"], 1)
                            dve.wait_ge(S["b0_ready"], 1)
                        else:
                            dve.wait_ge(S["b_ready"], n)
                        dve.wait_ge(S["a_done"], n + 1)
                        if n >= 2:
                            dve.wait_ge(S["g_done"], n - 1)
                        nc.vector.tensor_tensor_scan(h_sb[n % 2].rearrange(flat), a_sb[n % 2].rearrange(flat),
                                                     b_sb[n % 2].rearrange(flat), 0.0, ALU.mult, ALU.add)\
                            .then_inc(S["h_done"], 1)
                        dve.wait_ge(S["h_done"], n + 1)
                        dve.wait_ge(S["cn_mm"], n + 1)
                        if n >= 2:
                            dve.wait_ge(S["y_mm"], n - 1)
                        if n < NS - 1:
                            nc.vector.tensor_tensor(g_sb[n % 2], h_sb[n % 2],
                                                    bank(6 + n % 2).unsqueeze(1).to_broadcast([P, DT, T]), ALU.mult)\
                                .then_inc(S["g_done"], 1)
                    last = (NS - 1) % 2
                    for k in range(DT):
                        nc.vector.tensor_tensor(g_sb[last][:, k, :], h_sb[last][:, k, :], bank(6 + last), ALU.mult)\
                            .then_inc(S["g_last"], 1)
                    for k in range(DT):
                        dve.wait_ge(S["y_last"], k + 1)
                        link(nc.vector.scalar_tensor_tensor(delta[:, k, :], xs[:, k, :], D_skip[:, k:k + 1], bank(k),
                                                            ALU.mult, ALU.add))
                        nc.vector.tensor_tensor(u[:, k, :], delta[:, k, :], zs[:, k, :], ALU.mult)\
                            .then_inc(S["gated"], 1)

            TILES = [(x, hh, half) for hh in range(2) for x, half in ((0, 0), (1, 0), (2, 0), (3, 0), (3, 1))]
            LOAD_AFTER = {1: ((0,), 2), 2: ((1,), 3), 3: ((2,), 0), 5: ((3, 4), 1)}
            with nc.Block() as block:
                @block.sync
                def _(sp):
                    for i, (x, hh, half) in enumerate(TILES):
                        sp.wait_ge(S["parts_ready"], i + 1)
                        dst = qkv_dram[x, :, 8 * hh:8 * hh + 8, :, half * T:(half + 1) * T]
                        sp.dma_start(dst.rearrange("j h d t -> (h d) j t"), pt[i % NPT]).then_inc(parts_stored[i % NPT], 16)
                        if i == 1:
                            sp.wait_ge(S["outproj_mm"], TT)
                        if i in LOAD_AFTER:
                            tiles, operand = LOAD_AFTER[i]
                            for tile in tiles:
                                sp.wait_ge(parts_stored[tile], 16)
                            load_stack(sp, 0, operand)

                @block.tensor
                def _(pe):
                    pe.wait_ge(S["gated"], DT)
                    for t in range(TT):
                        for k in range(DT):
                            last = mm(bank(4 + t)[:, 0:DM], u[:, k, tok(t)], out_w[:, k, :], k == 0, k == DT - 1)
                        last.then_inc(S["outproj_mm"], 1)
                    to_columns(pe, xn, TT, 0)
                    pe.wait_ge(S["xT_ready"], 4)
                    pe.wait_ge(S["load_ctx"], 16)
                    ws = [wq, wk, wcq]
                    nv = [0]

                    def value_tile():
                        t = nv[0]
                        if t >= 2:
                            pe.wait_ge(S["v_ready"], t - 1)
                        o = bank(t % 2)[:, 0:DM]
                        if t < TT:
                            for k in range(KM):
                                last = mm(o, xT[:, k, tok(t)], wv[:, k, :], k == 0, k == KM - 1)
                        else:
                            last = mm(o, ctxT[:, tok(t - TT)], wcv[:], True, True)
                        last.then_inc(S["v_mm"], 1)
                        nv[0] += 1

                    for i, (x, hh, half) in enumerate(TILES):
                        if i >= 6:
                            pe.wait_ge(S["hi_f_ready"], i - 5)
                        o = bank(2 + i % 6)
                        cols = slice(hh * P, (hh + 1) * P)
                        if x < 3:
                            for k in range(KM):
                                last = mm(o, ws[x][:, k, cols], xT[:, k, :], k == 0, k == KM - 1)
                        else:
                            last = mm(o, wck[:, cols], ctxT[:, half * T:(half + 1) * T], True, True)
                        last.then_inc(S["qkv_mm"], 1)
                        value_tile()
                    value_tile()
                    value_tile()

                @block.scalar
                def _(act):
                    link = chain(act, S["act_chain3"])
                    act.wait_ge(S["xT_mm"], 4)
                    nc.scalar.activation(xT[:, 0, :], bank(0), ACT.Copy).then_inc(S["xT_ready"], 1)
                    for i, (x, hh, half) in enumerate(TILES):
                        act.wait_ge(S["qkv_mm"], i + 1)
                        if i >= NPT:
                            act.wait_ge(parts_stored[i % NPT], 16)
                        if i >= 2:
                            act.wait_ge(S["mid_ready"], i - 1)
                        bias = bqk[:, x, hh:hh + 1]
                        nc.scalar.activation(pt[i % NPT][:, 0, :], bank(2 + i % 6), ACT.Identity, bias=bias)
                        nc.scalar.activation(f_sb[i % 2], bank(2 + i % 6), ACT.Identity, bias=bias)\
                            .then_inc(S["hi_f_ready"], 1)

                @block.gpsimd
                def _(pool):
                    nc.gpsimd.memset(V, 0.0).then_inc(S["v_init"], 1)
                    nc.gpsimd.memset(VC, 0.0).then_inc(S["v_init"], 1)
                    pool.wait_ge(S["v_init"], 2)
                    nc.gpsimd.memset(V[:, :, :, HD:HD + 1], 1.0)
                    nc.gpsimd.memset(VC[:, :, :, HD:HD + 1], 1.0).then_inc(S["v_init"], 1)
                    pool.wait_ge(S["xn_ready"], 2 * TT)
                    nc.gpsimd.tensor_tensor(x1[:], x1[:], bp[:].unsqueeze(1).to_broadcast([P, TT, DM]), ALU.add)\
                        .then_inc(S["bp_added"], 1)
                    for i in range(len(TILES)):
                        pool.wait_ge(S["mid_ready"], i + 1)
                        nc.gpsimd.tensor_tensor(pt[i % NPT][:, 2, :], r_sb[i % 2], pt[i % NPT][:, 1, :], ALU.subtract)\
                            .then_inc(S["parts_ready"], 1)

                @block.vector
                def _(dve):
                    link = chain(dve, S["dve_chain3"])
                    def residual(t):
                        dve.wait_ge(S["outproj_mm"], t + 1)
                        link(nc.vector.tensor_tensor(x1[:, t, :], x_sb[:, t, :], bank(4 + t)[:, 0:DM], ALU.add))

                    normalise(dve, link, x1, xn, residual)
                    dve.wait_ge(S["xT_mm"], 4)
                    nc.vector.tensor_copy(xT[:, 1, :], bank(1)).then_inc(S["xT_ready"], 1)
                    dve.wait_ge(S["v_init"], 3)
                    nv = [0]

                    def value_tile():
                        t = nv[0]
                        dve.wait_ge(S["v_mm"], t + 1)
                        dst, bias = (V[:, t, :, 0:HD], bv) if t < TT else (VC[:, t - TT, :, 0:HD], bcv)
                        heads = "p (h d) -> p h d"
                        nc.vector.tensor_tensor(dst, bank(t % 2)[:, 0:DM].rearrange(heads, h=H),
                                                bias[:].rearrange(heads, h=H), ALU.add).then_inc(S["v_ready"], 1)
                        nv[0] += 1

                    for i in range(len(TILES)):
                        dve.wait_ge(S["hi_f_ready"], i + 1)
                        if i >= 2:
                            dve.wait_ge(S["parts_ready"], i - 1)
                        link(nc.vector.tensor_tensor(r_sb[i % 2], f_sb[i % 2], pt[i % NPT][:, 0, :], ALU.subtract))
                        nc.vector.tensor_copy(pt[i % NPT][:, 1, :], r_sb[i % 2]).then_inc(S["mid_ready"], 1)
                        value_tile()
                    value_tile()
                    value_tile()

            CS = 2 * TT
            STEPS = CS + TT
            CJOBS = HG * TT
            JOBS = CJOBS + HG * 2

            def ring(g, k, h):
                return HG * (STEPS * g + k) + h + 2 * max(g - 1, 0) + (2 if g >= 1 and k >= 2 else 0)

            def ring_den(g, i):
                return HG * STEPS * (g + 1) + 2 * g + i + (2 * HG if g + 1 < NG else 0)

            def max_slot(g, i):
                return i % 2 if g else (i + (1 if i >= CJOBS else 0)) % 4

            def all_stored(eng, bufs=range(NPT)):
                for i in bufs:
                    eng.wait_ge(parts_stored[i], 16 * len(range(i, len(TILES), NPT)))

            with nc.Block() as block:
                @block.sync
                def _(sp):
                    def load_max_rows(g, sides=(0, 1)):
                        for side in sides:
                            dst = (C, Q)[side]
                            sp.wait_ge(S["mparts_ready"], 2 * g + side + 1)
                            for j in range(3):
                                sp.dma_start(dst[g % NPAR][SK + j:SK + j + 1], mparts[:, side, j, :])\
                                    .then_inc(max_rows[g][side], 16)

                    all_stored(sp)
                    load_stacks(sp, 1)
                    load_max_rows(0, (0,))
                    load_stacks(sp, 2)
                    load_max_rows(0, (1,))
                    load_max_rows(1)
                    sp.wait_ge(S["pv_mm"], STEPS)
                    load_stacks(sp, 3)
                    load_max_rows(2)
                    load_max_rows(3)

                @block.gpsimd
                def _(pool):
                    all_stored(pool)
                    for i in range(NPAR):
                        nc.gpsimd.memset(K[i][SK:SR], 1.0).then_inc(S["ones_ready"], 1)
                        nc.gpsimd.memset(KC[i][SK:SR], 1.0).then_inc(S["ones_ready"], 1)
                    link = chain(pool, S["pool_chain4"])
                    for g in range(NG):
                        pool.wait_ge(S["ring_read"], ring_den(g, 1) + 1)
                        nc.gpsimd.tensor_tensor(R1, den_sb[:, 0, :], den_sb[:, 1, :], ALU.mult)\
                            .then_inc(S["den_ready"], 1)
                        nc.gpsimd.tensor_tensor(Y1, Y1, den_sb[:, 1, :], ALU.mult)
                        link(nc.gpsimd.tensor_tensor(Y2, Y2, den_sb[:, 0, :], ALU.mult))
                        link(nc.gpsimd.tensor_tensor(Y1, Y1, Y2, ALU.add))
                        pool.wait_ge(S["norm_ready"], g + 1)
                        nc.gpsimd.tensor_tensor(YT[g], Y1, R2, ALU.mult).then_inc(S["y_ready"], 1)

                @block.tensor
                def _(pe):
                    def max_job(g, i):
                        J = JOBS * g + i
                        h, r, par = (i // TT, i % TT, g % NPAR) if i < CJOBS else \
                            ((i - CJOBS) // 2, TT + i % 2, g % NPAR)
                        s = max_slot(g, i)
                        slots = 4 if g == 0 else 2
                        if J >= slots:
                            pe.wait_ge(S["max_done"], J + 1 - slots)
                        if i == 0 and g >= 1:
                            pe.wait_ge(S["mt_read"], 2 * g)
                        if i >= CJOBS and s == 0 and i < CJOBS + slots:
                            pe.wait_ge(S["mt_read"], 2 * g + 1)
                        if r < TT:
                            for c in range(2):
                                last = mm(bank(2 * s + c), C[par][0:SK, h, tok(r)],
                                          KC[par][0:SK, h, c * T:(c + 1) * T], True, True)
                        else:
                            for c, q in enumerate((3, 0) if r == TT else (2, 1)):
                                mm(bank(2 * s + c)[:, 0:(q + 1) * P], Q[par][0:SK, h, tok(q)],
                                   K[par][0:SK, h, 0:(q + 1) * P], True, False)
                                last = mm(bank(2 * s + c)[:, tok(q)], identb[:], mask_qk[:], False, True)
                        last.then_inc(S["max_mm"], 1)

                    def max_rows_out(g, side):
                        pe.wait_ge(S["max_done"], JOBS * g + (JOBS if side else CJOBS))
                        for q in range(TT):
                            last = nc.tensor.transpose(bank(0)[0:HG, tok(q)],
                                                       maxs[:, g % 2, q, side * HG:(side + 1) * HG], ident[:])
                        last.then_inc(S["mt_mm"], 1)

                    def scores(g, k, heads):
                        par = g % NPAR
                        for h in heads:
                            n = ring(g, k, h)
                            if n >= 2:
                                pe.wait_ge(S["ring_read"], n - 1)
                            o = bank(4 + n % 2)
                            if k < CS:
                                last = mm(o, KC[par][0:SR, h, tok(k)], C[par][0:SR, h, :], True, True)
                            else:
                                kt = k - CS
                                mm(o[:, 0:T - kt * P], K[par][0:SR, h, tok(kt)], Q[par][0:SR, h, kt * P:T],
                                   True, False)
                                last = mm(o[:, 0:P], identb[:], mask_kq[:], False, True)
                            last.then_inc(S["ring_mm"], 1)

                    def denominators(g):
                        pe.wait_ge(S["pv_copied"], g + 1)
                        for i, y in enumerate((Y1, Y2)):
                            pe.wait_ge(S["ring_read"], ring_den(g, i) - 1)
                            mm(bank(4 + ring_den(g, i) % 2), den_sel[:], y, True, True).then_inc(S["ring_mm"], 1)

                    def values(g, k):
                        pe.wait_ge(S["ring_read"], ring(g, k, HG - 1) + 1)
                        if k == 0 and g >= 1:
                            pe.wait_ge(S["pv_copied"], g)
                        for h in range(HG):
                            n = HG * (STEPS * g + k) + h
                            rows = slice(32 * h, 32 * h + VW)
                            if k < CS:
                                last = mm(bank(6)[rows], VC[:, k, HG * g + h, :], probs[n % NPR], k == 0, k == CS - 1)
                            else:
                                kt = k - CS
                                last = mm(bank(7)[rows, kt * P:T], V[:, kt, HG * g + h, :],
                                          probs[n % NPR][:, 0:T - kt * P], kt == 0, kt == TT - 1)
                        last.then_inc(S["pv_mm"], 1)

                    n_stack = 16 * 4 * 6
                    pe.wait_ge(stack_in[0], n_stack)
                    for i in range(JOBS):
                        if i == CJOBS:
                            max_rows_out(0, 0)
                        max_job(0, i)
                    pe.wait_ge(S["max_done"], JOBS)
                    pe.wait_ge(S["ones_ready"], 2 * NPAR)
                    for g in range(NG):
                        pe.wait_ge(max_rows[g][0], 16 * 3)
                        if g + 1 < NG:
                            pe.wait_ge(stack_in[g + 1], n_stack)
                        job = 0
                        for k in range(STEPS):
                            if k == CS:
                                pe.wait_ge(max_rows[g][1], 16 * 3)
                            scores(g, k, (0, 1))
                            if k == 0:
                                max_rows_out(g, 1)
                            late = k == 0 or job == CJOBS
                            if g + 1 < NG:
                                if job == CJOBS:
                                    max_rows_out(g + 1, 0)
                                if not late:
                                    max_job(g + 1, job)
                            scores(g, k, (2, 3))
                            if g + 1 < NG and not late:
                                max_job(g + 1, job + 1)
                            if k == 1 and g >= 1:
                                denominators(g - 1)
                            if k >= 1:
                                values(g, k - 1)
                            elif g >= 1:
                                values(g - 1, STEPS - 1)
                            if g + 1 < NG:
                                if late:
                                    max_job(g + 1, job)
                                    max_job(g + 1, job + 1)
                                job += 2
                    values(NG - 1, STEPS - 1)
                    denominators(NG - 1)

                @block.scalar
                def _(act):
                    def copy_sums(g):
                        act.wait_ge(S["pv_mm"], STEPS * (g + 1))
                        if g >= 1:
                            act.wait_ge(S["y_ready"], g)
                        nc.scalar.activation(Y1, bank(6), ACT.Copy)
                        nc.scalar.activation(Y2, bank(7), ACT.Copy).then_inc(S["pv_copied"], 1)

                    def copy_denominators(g):
                        for i in range(2):
                            n = ring_den(g, i)
                            act.wait_ge(S["ring_mm"], n + 1)
                            nc.scalar.activation(den_sb[:, i, :], bank(4 + n % 2), ACT.Copy)\
                                .then_inc(S["ring_read"], 1)

                    all_stored(act, range(4, NPT))
                    for i in range(CJOBS):
                        act.wait_ge(S["max_mm"], i + 1)
                        if i >= 4:
                            act.wait_ge(S["max_done"], i - 3)
                        nc.scalar.activation(probs[i % 4], bank(2 * max_slot(0, i) + 1), ACT.Copy).then_inc(S["half_ready"], 1)
                    act.wait_ge(S["max_done"], CJOBS)
                    for s in range(NG * STEPS):
                        g, k = s // STEPS, s % STEPS
                        N = T if k < CS else T - (k - CS) * P
                        if s >= 2:
                            act.wait_ge(S["pv_mm"], s - 1)
                        for h in range(HG):
                            n = ring(g, k, h)
                            act.wait_ge(S["ring_mm"], n + 1)
                            nc.scalar.activation(probs[(HG * s + h) % NPR][:, 0:N], bank(4 + n % 2)[:, 0:N], ACT.Exp,
                                                 scale=HD ** -0.5).then_inc(S["ring_read"], 1)
                        if g >= 1 and k == 0:
                            copy_sums(g - 1)
                        if g >= 1 and k == 1:
                            copy_denominators(g - 1)
                    copy_sums(NG - 1)
                    copy_denominators(NG - 1)

                @block.vector
                def _(dve):
                    link = chain(dve, S["dve_chain4"])

                    def maxima(g, jobs):
                        for i in jobs:
                            J = JOBS * g + i
                            h, r = (i // TT, i % TT) if i < CJOBS else ((i - CJOBS) // 2, TT + i % 2)
                            s = max_slot(g, i)
                            dve.wait_ge(S["max_mm"], J + 1)
                            if r < TT and g == 0:
                                dve.wait_ge(S["half_ready"], i + 1)
                                if i >= TT:
                                    dve.wait_ge(S["max_done"], i // TT * TT)
                                last = nc.vector.tensor_tensor_scan(running[:, r, :], bank(2 * s), probs[i % 4],
                                                                    -3.0e38, ALU.max, ALU.max)
                                if r == TT - 1:
                                    link(last)
                                    last = nc.vector.tensor_copy(maxs[:, 0, :, h:h + 1], running[:, :, T - 1:T])
                            elif r < TT:
                                last = nc.vector.reduce_max(maxs[:, g % 2, r, h:h + 1],
                                                            PS[:, 2 * s:2 * s + 2, :].rearrange("p a n -> p (a n)"), AXX)
                            else:
                                for c_, q in enumerate((3, 0) if r == TT else (2, 1)):
                                    last = nc.vector.reduce_max(maxs[:, g % 2, q, HG + h:HG + h + 1],
                                                                bank(2 * s + c_)[:, 0:(q + 1) * P], AXX)
                            last.then_inc(S["max_done"], 1)

                    def negated_parts(g, side):
                        dve.wait_ge(S["mt_mm"], 2 * g + side + 1)
                        if g >= 1:
                            dve.wait_ge(max_rows[g - 1][side], 16 * 3)
                        if g + side >= 1:
                            dve.wait_ge(S["mparts_ready"], 2 * g + side)
                        m = mparts[:, side]
                        src = bank(0)[0:HG]
                        link(nc.vector.tensor_scalar(m[:, 0, :], src, -1.0, None, ALU.mult))
                        nc.vector.scalar_tensor_tensor(mrest[:], src, -1.0, m[:, 0, :], ALU.mult, ALU.subtract)\
                            .then_inc(S["mt_read"], 1)
                        dve.wait_ge(S["mt_read"], 2 * g + side + 1)
                        link(nc.vector.tensor_copy(m[:, 1, :], mrest[:]))
                        nc.vector.tensor_tensor(m[:, 2, :], mrest[:], m[:, 1, :], ALU.subtract)\
                            .then_inc(S["mparts_ready"], 1)

                    def invert(g):
                        dve.wait_ge(S["den_ready"], g + 1)
                        nc.vector.reciprocal(R2, R1).then_inc(S["norm_ready"], 1)

                    maxima(0, range(CJOBS))
                    negated_parts(0, 0)
                    maxima(0, range(CJOBS, JOBS))
                    for g in range(NG):
                        negated_parts(g, 1)
                        if g + 1 < NG:
                            maxima(g + 1, range(8))
                        if g >= 1:
                            invert(g - 1)
                        if g + 1 < NG:
                            maxima(g + 1, range(8, CJOBS))
                            negated_parts(g + 1, 0)
                            maxima(g + 1, range(CJOBS, JOBS))
                    invert(NG - 1)

            with nc.Block() as block:
                @block.sync
                def _(sp):
                    for e in range(NE):
                        sp.dma_start(ew1[e], w["ew1"][e].rearrange("(k p) n -> p k n", p=P)).then_inc(load_e[e], 16)
                        sp.dma_start(ew2[e], w["ew2"][e].rearrange("(k p) n -> p k n", p=P)).then_inc(load_e[e], 16)
                    for t in range(0, TT, 2):
                        sp.wait_ge(S["out_ready"], t + 2)
                        sp.dma_start(out[bass.ds(b, 1), t * P:(t + 2) * P, :].rearrange("a (t p) n -> p (a t) n", p=P),
                                     mixed[:, t:t + 2, :]).then_inc(S["stored"], 16)
                    sp.wait_ge(S["stored"], 16 * TT // 2)

                @block.gpsimd
                def _(pool):
                    pool.wait_ge(S["xn_ready"], 3 * TT)
                    nc.gpsimd.tensor_tensor(x1[:], x1[:], xn[:], ALU.add).then_inc(S["res_added"], 1)
                    pool.wait_ge(S["res_added"], 1)
                    pool.wait_ge(S["abel_ready"], 1)
                    nc.gpsimd.tensor_tensor(x1[:], x1[:], ab[:, :, 0:DM], ALU.add).then_inc(S["res_added"], 1)

                @block.tensor
                def _(pe):
                    for t in range(TT):
                        for g in range(NG):
                            last = mm(bank(t)[:, 0:DM], YT[g][:, tok(t)], wp[:, g, :], g == 0, g == NG - 1)
                        last.then_inc(S["wp_mm"], 1)
                    to_columns(pe, xn2, 3 * TT, 4)
                    pe.wait_ge(S["xT_ready"], 6)
                    for t in range(TT):
                        for k in range(KM):
                            last = mm(bank(t)[:, 0:DM + NE], xT[:, k, tok(t)], abw[:, k, :], k == 0, k == KM - 1)
                        last.then_inc(S["ab_mm"], 1)

                    def hidden(e):
                        pe.wait_ge(load_e[e], 32)
                        for m in range(HT):
                            i = HT * e + m
                            if e == 0:
                                pe.wait_ge(S["abel_pre"], m + 1)
                            else:
                                pe.wait_ge(S["hid_ready"], i - HT + 1)
                            for k in range(KM):
                                last = mm(bank(m), ew1[e][:, k, m * P:(m + 1) * P], xT[:, k, :], k == 0, k == KM - 1)
                            last.then_inc(S["hid_mm"], 1)

                    def output(e):
                        pe.wait_ge(S["hid_ready"], HT * (e + 1))
                        if e == 1:
                            pe.wait_ge(S["moe_init"], 1)
                        if e >= 2:
                            pe.wait_ge(S["eo_added"], e - 1)
                        for t in range(TT):
                            for k in range(HT):
                                o = bank(4 + 2 * (e % 2) + t // 2)[:, (t % 2) * DM:(t % 2 + 1) * DM]
                                last = mm(o, hid[e % 2][:, k, tok(t)], ew2[e][:, k, :], k == 0, k == HT - 1)
                        last.then_inc(S["eo_mm"], 1)

                    hidden(0)
                    pe.wait_ge(S["sel_ready"], 1)
                    for t in range(TT):
                        last = nc.tensor.transpose(bank(6)[0:NE, tok(t)], sel[:, t, :], ident[:])
                    last.then_inc(S["wT_mm"], 1)
                    hidden(1)
                    pe.wait_ge(S["wT_ready"], 1)
                    for t in range(TT):
                        last = mm(bank(6 + t // 2)[:, (t % 2) * DM:(t % 2 + 1) * DM], selT[:, tok(t)], eb2[:], True, True)
                    last.then_inc(S["eb_mm"], 1)
                    for e in range(NE):
                        output(e)
                        if e + 2 < NE:
                            hidden(e + 2)
                    pe.wait_ge(S["eo_added"], NE)
                    for t in range(TT):
                        for k in range(KM):
                            last = nc.tensor.transpose(bank(k)[:, tok(t)], acc[:, t, k * P:(k + 1) * P], ident[:])
                    last.then_inc(S["moeT_mm"], 1)
                    pe.wait_ge(S["moeT_ready"], 2)
                    for t in range(TT):
                        for k in range(KM):
                            last = mm(bank(4 + t)[:, 0:DM], moeT[:, k, tok(t)], Wrot[:, k, :], k == 0, k == KM - 1)
                        last.then_inc(S["rot_mm"], 1)

                @block.scalar
                def _(act):
                    link = chain(act, S["act_chain5"])
                    act.wait_ge(S["xT_mm"], 6)
                    nc.scalar.activation(xT[:, 0, :], bank(4), ACT.Identity, bias=bet[:, 0:1], scale=gam[:, 0:1])\
                        .then_inc(S["xT_ready"], 1)
                    act.wait_ge(S["sel_d"], 2)
                    nc.scalar.activation(sel_ex[:], sel_ex[:], ACT.Exp).then_inc(S["sel_e"], 1)
                    nc.scalar.activation(sel_e2[:], sel_e2[:], ACT.Exp).then_inc(S["sel_e"], 1)
                    for e in range(NE):
                        for m in range(HT):
                            act.wait_ge(S["hid_mm"], HT * e + m + 1)
                            if e >= 2:
                                act.wait_ge(S["eo_mm"], e - 1)
                            nc.scalar.activation(hid[e % 2][:, m, :], bank(m), ACT.Gelu, bias=eb1[:, e, m:m + 1])\
                                .then_inc(S["hid_ready"], 1)
                        if e == 1:
                            nc.scalar.activation(ab[:, :, 0:DM], ab[:, :, 0:DM], ACT.Gelu).then_inc(S["abel_ready"], 1)
                    act.wait_ge(S["moeT_mm"], 1)
                    nc.scalar.activation(moeT[:, 0, :], bank(0), ACT.Copy).then_inc(S["moeT_ready"], 1)
                    act.wait_ge(S["gate_z"], 1)
                    nc.scalar.activation(gate[:, 1, :], gate[:, 0, :], ACT.Exp, scale=-1.0).then_inc(S["gate_e"], 1)

                @block.vector
                def _(dve):
                    link = chain(dve, S["dve_chain5"])
                    def residual(t):
                        dve.wait_ge(S["wp_mm"], t + 1)
                        link(nc.vector.tensor_tensor(x1[:, t, :], x1[:, t, :], bank(t)[:, 0:DM], ALU.add))

                    normalise(dve, link, x1, xn, residual)
                    dve.wait_ge(S["xn_ready"], 3 * TT)
                    normalise(dve, link, xn, xn2)
                    dve.wait_ge(S["xT_mm"], 6)
                    nc.vector.tensor_scalar(xT[:, 1, :], bank(5), gam[:, 1:2], bet[:, 1:2], ALU.mult, ALU.add)\
                        .then_inc(S["xT_ready"], 1)
                    for t in range(TT):
                        dve.wait_ge(S["ab_mm"], t + 1)
                        nc.vector.tensor_tensor(ab[:, t, :], bank(t)[:, 0:DM + NE], abb[:], ALU.add)\
                            .then_inc(S["abel_pre"], 1)
                    dve.wait_ge(S["abel_pre"], TT)
                    lg = ab[:, :, DM:DM + NE]
                    for t in range(TT):
                        link(nc.vector.max(m8[:, t, :], ab[:, t, DM:DM + NE]))
                    m1, m2 = m8[:, :, 0:1], m8[:, :, 1:2]

                    def over(v):
                        return v.to_broadcast([P, TT, NE])

                    nc.vector.tensor_tensor(sel_ex[:], lg, over(m1), ALU.subtract).then_inc(S["sel_d"], 1)
                    nc.vector.tensor_tensor(sel_e2[:], m2, m1, ALU.subtract).then_inc(S["sel_d"], 1)
                    link(nc.vector.tensor_tensor(s_gt[:], lg, over(m2), ALU.is_gt))
                    link(nc.vector.tensor_tensor(s_eq[:], lg, over(m2), ALU.is_equal))
                    link(nc.vector.tensor_tensor(s_one[:], m1, m2, ALU.is_gt))
                    link(nc.vector.memset(s_zero[:], 0.0))
                    for t in range(TT):
                        link(nc.vector.tensor_tensor_scan(sel[:, t, :], s_eq[:, t, :], s_zero[:], 0.0,
                                                          ALU.add, ALU.add))
                    link(nc.vector.tensor_tensor(sel[:], sel[:], over(s_one[:]), ALU.add))
                    link(nc.vector.scalar_tensor_tensor(sel[:], sel[:], 2.0, s_eq[:], ALU.is_le, ALU.mult))
                    link(nc.vector.tensor_tensor(sel[:], sel[:], s_gt[:], ALU.add))
                    dve.wait_ge(S["sel_e"], 2)
                    link(nc.vector.tensor_scalar(s_den[:], sel_e2[:], 1.0, None, ALU.add))
                    link(nc.vector.reciprocal(s_den[:], s_den[:]))
                    link(nc.vector.tensor_tensor(sel[:], sel[:], sel_ex[:], ALU.mult))
                    nc.vector.tensor_tensor(sel[:], sel[:], over(s_den[:]), ALU.mult).then_inc(S["sel_ready"], 1)
                    dve.wait_ge(S["wT_mm"], 1)
                    nc.vector.tensor_copy(selT[:], bank(6)[0:NE]).then_inc(S["wT_ready"], 1)
                    dve.wait_ge(S["eb_mm"], 1)
                    nc.vector.tensor_copy(acc.rearrange("p t n -> p (t n)"),
                                          PS[:, 6:8, :].rearrange("p a n -> p (a n)")).then_inc(S["moe_init"], 1)
                    dve.wait_ge(S["moe_init"], 1)
                    dve.wait_ge(S["sel_ready"], 1)
                    for e in range(NE):
                        dve.wait_ge(S["eo_mm"], e + 1)
                        if e >= 1:
                            dve.wait_ge(S["eo_added"], e)
                        for t in range(TT):
                            o = bank(4 + 2 * (e % 2) + t // 2)[:, (t % 2) * DM:(t % 2 + 1) * DM]
                            last = nc.vector.scalar_tensor_tensor(acc[:, t, :], o, sel[:, t, e:e + 1], acc[:, t, :],
                                                                  ALU.mult, ALU.add)
                        last.then_inc(S["eo_added"], 1)
                    dve.wait_ge(S["moeT_mm"], 1)
                    nc.vector.tensor_copy(moeT[:, 1, :], bank(1)).then_inc(S["moeT_ready"], 1)
                    dve.wait_ge(S["abel_ready"], 1)
                    for t in range(TT):
                        link(nc.vector.tensor_tensor_reduce(out=mixed[:, t, :], in0=ab[:, t, 0:DM], in1=gcw[:, 0:DM],
                                                            scale=1.0, scalar=0.0, op0=ALU.mult, op1=ALU.add,
                                                            accum_out=gate[:, 2, t:t + 1]))
                    for t in range(TT):
                        dve.wait_ge(S["rot_mm"], t + 1)
                        link(nc.vector.tensor_tensor_reduce(out=mixed[:, t, :], in0=bank(4 + t)[:, 0:DM],
                                                            in1=gcw[:, DM:2 * DM], scale=1.0, scalar=0.0,
                                                            op0=ALU.mult, op1=ALU.add, accum_out=gate[:, 0, t:t + 1]))
                    link(nc.vector.tensor_tensor(gate[:, 0, :], gate[:, 0, :], gate[:, 2, :], ALU.add))
                    nc.vector.tensor_scalar(gate[:, 0, :], gate[:, 0, :], gcb[:, 0:1], -80.0, ALU.add, ALU.max)\
                        .then_inc(S["gate_z"], 1)
                    for t in range(TT):
                        last = nc.vector.tensor_tensor(diff[:, t, :], bank(4 + t)[:, 0:DM], ab[:, t, 0:DM],
                                                       ALU.subtract)
                    link(last)
                    dve.wait_ge(S["gate_e"], 1)
                    link(nc.vector.tensor_scalar(gate[:, 1, :], gate[:, 1, :], 1.0, None, ALU.add))
                    link(nc.vector.reciprocal(gate[:, 1, :], gate[:, 1, :]))
                    dve.wait_ge(S["res_added"], 2)
                    for t in range(TT):
                        nc.vector.scalar_tensor_tensor(mixed[:, t, :], diff[:, t, :], gate[:, 1, t:t + 1],
                                                       x1[:, t, :], ALU.mult, ALU.add).then_inc(S["out_ready"], 1)
            reset()


def kernel(**inputs):
    import numpy as np
    import concourse.bacc as bacc
    from concourse.bass_utils import run_bass_kernel_spmd

    attn = {n: np.asarray(inputs["L0_attn_" + n]) for n in
            ("in_proj_w", "conv_w", "conv_b", "x_proj_w", "dt_proj_w", "dt_proj_b", "A_log", "D", "out_proj_w")}
    arrays = {
        "in_proj_wT": attn["in_proj_w"].T, "conv_w": attn["conv_w"][:, 0, :], "conv_b": attn["conv_b"],
        "x_proj_wT": attn["x_proj_w"].T, "dt_proj_wT": attn["dt_proj_w"].T, "dt_proj_b": attn["dt_proj_b"],
        "A_log": attn["A_log"], "D": attn["D"], "out_proj_wT": attn["out_proj_w"].T,
    }
    for n in ("Wk", "bk", "Wq", "bq", "Wv", "bv", "Wck", "bck", "Wcq", "bcq", "Wcv", "bcv", "Wp", "bp"):
        arrays[n] = np.asarray(inputs["L0_xattn_" + n])
    for n in ("ln_gamma", "ln_beta", "abel_w", "abel_b", "moe_gate_w", "moe_gate_b", "ew1", "eb1", "ew2", "eb2",
              "gens", "gc_w", "gc_b"):
        arrays[n] = np.asarray(inputs["L0_ffn_" + n])
    for n in ("conv_b", "dt_proj_b", "D", "bq", "bk", "bcq", "bck", "ln_gamma", "ln_beta"):
        arrays[n] = arrays[n].reshape(-1, P).T
    arrays["eb1"] = arrays["eb1"].reshape(NE, HT, P).transpose(2, 0, 1)
    arrays["x"] = np.asarray(inputs["x"])
    arrays["ctx_t"] = np.asarray(inputs["ctx_512"]).transpose(0, 2, 1)

    nc = bacc.Bacc("TRN2", target_bir_lowering=False, num_devices=1)
    feed, aps = {}, {}
    for name, a in arrays.items():
        a = np.ascontiguousarray(a)
        feed[f"in_{name}"] = a
        aps[name] = nc.dram_tensor(f"in_{name}", a.shape, mybir.dt.from_np(a.dtype), kind="ExternalInput").ap()
    out = nc.dram_tensor("out", (NB, T, DM), F32, kind="ExternalOutput").ap()
    decoder(nc, aps, aps["x"], aps["ctx_t"], out)
    r = run_bass_kernel_spmd(nc, [feed], core_ids=[0])
    return r.results[0]["out"]
```
